# Optimizing a Trainium2 kernel written in Bass

```python
import numpy as np
import jax
import jax.numpy as jnp

def _softmax(x, axis=-1):
    return jax.nn.softmax(x, axis=axis)

def _gelu(x):
    return jax.nn.gelu(x, approximate=True)

def _silu(x):
    return jax.nn.silu(x)

def _sigmoid(x):
    return jax.nn.sigmoid(x)

def _layernorm(x, axis=-1, eps=1e-05):
    m = jnp.mean(x, axis=axis, keepdims=True)
    v = jnp.var(x, axis=axis, keepdims=True)
    return (x - m) / jnp.sqrt(v + eps)

def _scatter_add(tgt, idx, src, axis=0):
    return tgt.at[idx].add(src)

def _segment_sum(src, seg, n):
    return jax.ops.segment_sum(src, seg, n)
kernel_name = 'mk_adj_preln_d1_adj_r2_a7cd4d'

def setup_inputs(seed: int=0):
    np.random.seed(seed)
    _w = jnp.asarray

    def _rec_inputs():
        import jax
        import jax.numpy as jnp
        _gk = jax.random.key(seed)
        x = -9.806e-05 + 1 * jax.random.normal(jax.random.fold_in(_gk, 1), (8192, 128), jnp.float32)
        _a = jax.random.bernoulli(jax.random.fold_in(_gk, 2), 0.000488281, (8192, 8192))
        _a = jnp.logical_or(_a, jnp.eye(8192, dtype=bool))
        _af = _a.astype(jnp.float32)
        adj = _af
        return (x, adj)
    x, adj = _rec_inputs()

    def _L0_gnn_setup():
        import jax, jax.numpy as jnp
        import numpy as np
        N, F_IN, HEADS, F_OUT = (2048, 128, 4, 32)
        DENSITY = 0.05
        key = jax.random.key(seed)
        k_x, k_adj, k_w, k_as, k_ad, k_b = jax.random.split(key, 6)
        x = jax.random.normal(k_x, (N, F_IN), dtype=jnp.float32)
        adj = (jax.random.uniform(k_adj, (N, N)) < DENSITY).astype(jnp.float32)
        adj = jnp.maximum(adj, jnp.eye(N, dtype=jnp.float32))
        weight = jax.random.normal(k_w, (HEADS * F_OUT, F_IN), dtype=jnp.float32) * 0.1
        att_src = jax.random.normal(k_as, (1, HEADS, F_OUT), dtype=jnp.float32) * 0.1
        att_dst = jax.random.normal(k_ad, (1, HEADS, F_OUT), dtype=jnp.float32) * 0.1
        bias = jax.random.normal(k_b, (HEADS * F_OUT,), dtype=jnp.float32) * 0.1
        return {'x': x, 'adj_matrix': adj, 'weight': weight, 'att_src': att_src, 'att_dst': att_dst, 'bias': bias}
    _L0_gnn_all = _L0_gnn_setup()
    _L0_gnn_in = {k: v for k, v in _L0_gnn_all.items() if k in ('weight', 'att_src', 'att_dst', 'bias')}
    del _L0_gnn_all
    return {'x': x, 'adj': adj, 'L0_gnn_weight': _L0_gnn_in['weight'], 'L0_gnn_att_src': _L0_gnn_in['att_src'], 'L0_gnn_att_dst': _L0_gnn_in['att_dst'], 'L0_gnn_bias': _L0_gnn_in['bias']}

def reference(x, adj, L0_gnn_weight, L0_gnn_att_src, L0_gnn_att_dst, L0_gnn_bias):
    import jax
    import jax.numpy as jnp

    def _L0_gnn_ref(x, adj_matrix, weight, att_src, att_dst, bias):
        import jax, jax.numpy as jnp
        import numpy as np
        N, F_IN, HEADS, F_OUT = (2048, 128, 4, 32)
        DENSITY = 0.05
        n = x.shape[0]
        heads = att_src.shape[1]
        f_out = weight.shape[0] // heads
        h_prime = (x @ weight.T).reshape(n, heads, f_out)
        alpha_src = jnp.sum(h_prime * att_src, axis=-1)
        alpha_dst = jnp.sum(h_prime * att_dst, axis=-1)
        C = alpha_src[None, :, :] + alpha_dst[:, None, :]
        adj_t = adj_matrix.T[..., None]
        tau = adj_t * jnp.exp(jnp.maximum(0.2 * C, C))
        tau_sum = jnp.sum(tau, axis=1, keepdims=True)
        att_weights = tau / tau_sum
        z = jnp.einsum('mnh,nhf->mhf', adj_t * att_weights, h_prime)
        return z.reshape(n, heads * f_out) + bias
    h = jnp.maximum(_layernorm(x, axis=-1), 0.0)
    x = x + _L0_gnn_ref(h, adj, L0_gnn_weight, L0_gnn_att_src, L0_gnn_att_dst, L0_gnn_bias)
    return x

_drawn_inputs = setup_inputs


def setup_inputs(seed=0):
    import zlib

    import numpy as np

    out = dict(_drawn_inputs(seed))
    spreads = {}
    factors = {}
    for name, (base, spread) in spreads.items():
        noise = np.random.default_rng([zlib.crc32(name.encode()), seed]).standard_normal(out[name].shape)
        drawn = base * np.exp(spread * noise) if base else spread * noise
        out[name] = jnp.asarray(drawn.astype(out[name].dtype))
    for name, factor in factors.items():
        out[name] = (out[name] * factor).astype(out[name].dtype)
    return out
```

```python
from contextlib import ExitStack

import concourse.bass as bass
from concourse import mybir

F32 = mybir.dt.float32
ALU = mybir.AluOpType
ACT = mybir.ActivationFunctionType
AX_X = mybir.AxisListType.X

P = 128
HEADS = 4
EPS = 1e-5
SLOPE = 0.2


def gat_kernel(nc, x, adj, weight, att_src, att_dst, bias, consts, out):
    N, F = x.shape
    T = N // P
    FO = F // HEADS
    HC = FO + 1
    VAL = HEADS * HC
    ROW = VAL + HEADS
    PG = 4
    GROUPS = T // PG
    CH = 8
    CHUNKS = T // CH

    table = nc.dram_tensor("node_table", (N, ROW), F32, kind="Internal").ap()

    with ExitStack() as ctx:
        def sb(name, shape, dt=F32):
            return ctx.enter_context(nc.sbuf_tensor(name, shape, dt))

        def psum(name, shape, dt=F32):
            return ctx.enter_context(nc.psum_tensor(name, shape, dt))

        def sem(name):
            return ctx.enter_context(nc.semaphore(name))

        const_sb = sb("const_sb", [P, P])
        ident = const_sb[:, 0:P]
        ones = sb("ones", [P, P])
        w_sb = sb("w_sb", [P, F])
        att_col = sb("att_col", [P, 2])
        att_block = sb("att_block", [P, 2 * HEADS])
        w_ext = sb("w_ext", [F, F + 2 * HEADS])
        bias_sb = sb("bias_sb", [P, F])
        alpha_dst = sb("alpha_dst", [P, T, HEADS])

        x_in = sb("x_in", [P, 2, PG, F])
        stats = sb("stats", [P, PG, 6])
        moments = sb("moments", [P, PG, 2])
        rstd = sb("rstd", [P, PG])
        x_norm = sb("x_norm", [P, PG, F])
        h_T = sb("h_T", [P, PG * P])
        rows = sb("rows", [P, 2, PG, ROW])

        adj_blk = sb("adj_blk", [P, 2, CH, P])
        src_rows = sb("src_rows", [P, 2, CH, ROW])
        dst_diag = sb("dst_diag", [P, HEADS, P])
        dst_bc = sb("dst_bc", [P, HEADS, P])
        tau = sb("tau", [P, CH, HEADS, P])
        tau_flat = tau[:, :, :, :].rearrange("p a b c -> p (a b c)")
        acc = sb("acc", [P, VAL])
        rden = sb("rden", [P, HEADS])
        x_res = sb("x_res", [P, F])
        z_out = sb("z_out", [P, F])

        ps_a = psum("ps_a", [P, 512])
        ps_b = psum("ps_b", [P, 2, 512])
        ps_c = psum("ps_c", [P, 512])

        names = ["sq", "consts_in", "setup", "w_turned", "w_kept", "w_cols", "x_loaded", "stats_done", "moments_done",
                 "rstd_done", "normed", "turned", "relued", "projected", "rows_kept", "rows_stored",
                 "adj_in0", "adj_in1", "src_in0", "src_in1", "diag_made", "bc_done", "bc_kept", "dv", "exp_done",
                 "tau_done", "mm_done", "acc_done", "res_in", "fin_done", "out_stored", "x_in0", "x_in1", "rows_st0", "rows_st1"]
        S = {n: sem("s_" + n) for n in names}

        block = ctx.enter_context(nc.Block())

        @block.sync
        def _(sp):
            sp.dma_start(const_sb[:, :], consts).then_inc(S["consts_in"], 16)
            sp.dma_start(w_sb[:, :], weight).then_inc(S["consts_in"], 16)
            sp.dma_start(att_col[:, 0:1], att_src.rearrange("a h f -> (h f) a")).then_inc(S["consts_in"], 16)
            sp.dma_start(att_col[:, 1:2], att_dst.rearrange("a h f -> (h f) a")).then_inc(S["consts_in"], 16)
            sp.dma_start(bias_sb[:, :], bias.rearrange("(a f) -> a f", a=1).to_broadcast([P, F])).then_inc(S["consts_in"], 16)
            for g in range(GROUPS):
                if g >= 2:
                    sp.wait_ge(S["normed"], g - 1)
                sp.dma_start(x_in[:, g % 2], x[g * PG * P:(g + 1) * PG * P, :].rearrange("(a p) f -> p a f", p=P)
                             ).then_inc(S[f"x_in{g % 2}"], 16)
            sp.wait_ge(S["rows_st0"], 16 * GROUPS // 2)
            sp.wait_ge(S["rows_st1"], 16 * GROUPS // 2)
            with sp.Fori(0, T) as m:
                for c in range(CHUNKS):
                    if c < 2:
                        sp.wait_ge(S["mm_done"], m * CHUNKS)
                    else:
                        sp.wait_ge(S["mm_done"], m * CHUNKS + (c - 1))
                    sp.dma_start(adj_blk[:, c % 2], adj[c * CH * P:(c + 1) * CH * P, bass.ds(m * P, P)]
                                 .rearrange("(a p) f -> p a f", p=P)).then_inc(S[f"adj_in{c % 2}"], 16)
                    sp.dma_start(src_rows[:, c % 2], table[c * CH * P:(c + 1) * CH * P, :]
                                 .rearrange("(a p) f -> p a f", p=P)).then_inc(S[f"src_in{c % 2}"], 16)
                sp.dma_start(x_res[:, :], x[bass.ds(m * P, P), :]).then_inc(S["res_in"], 16)
                sp.wait_ge(S["fin_done"], m + 1)
                sp.dma_start(out[bass.ds(m * P, P), :], z_out[:, :]).then_inc(S["out_stored"], 16)
            sp.wait_ge(S["out_stored"], 16 * T)

        @block.gpsimd
        def _(pool):
            pass

        @block.tensor
        def _(pe):
            pe.wait_ge(S["setup"], 1)
            pe.wait_ge(S["consts_in"], 80)
            pe.transpose(ps_a[:, 0:F], w_sb[:, :], ident)
            pe.matmul(ps_a[:, F:F + 2 * HEADS], w_sb[:, :], att_block[:, :], start=True, stop=True).then_inc(S["w_cols"], 1)
            for g in range(GROUPS):
                pe.wait_ge(S["normed"], g + 1)
                if g == 0:
                    pe.wait_ge(S["w_kept"], 1)
                else:
                    pe.wait_ge(S["relued"], g)
                for a in range(PG):
                    last = pe.transpose(ps_a[:, a * P:(a + 1) * P], x_norm[:, a, :], ident)
                last.then_inc(S["turned"], 1)
                pe.wait_ge(S["relued"], g + 1)
                if g >= 1:
                    pe.wait_ge(S["rows_kept"], g)
                for a in range(PG):
                    last = pe.matmul(ps_b[:, a // 2, (a % 2) * 136:(a % 2) * 136 + 136], h_T[:, a * P:(a + 1) * P],
                                     w_ext[:, :], start=True, stop=True)
                last.then_inc(S["projected"], 1)
            pe.wait_ge(S["rows_kept"], GROUPS)
            with pe.Fori(0, T) as m:
                pe.wait_ge(S["diag_made"], m + 1)
                pe.matmul(ps_a[:, :], ones[:, :], dst_diag[:, :, :].rearrange("p a b -> p (a b)"), start=True, stop=True).then_inc(S["bc_done"], 1)
                for c in range(CHUNKS):
                    pe.wait_ge(S["tau_done"], m * CHUNKS + (c + 1))
                    pe.wait_ge(S["acc_done"], m * CHUNKS + c) if c else pe.wait_ge(S["acc_done"], m * CHUNKS)
                    for h in range(HEADS):
                        for t in range(CH):
                            last = pe.matmul(ps_c[:, h * HC:(h + 1) * HC], tau[:, t, h, :],
                                             src_rows[:, c % 2, t, h * HC:(h + 1) * HC], start=(t == 0), stop=(t == CH - 1))
                    last.then_inc(S["mm_done"], 1)

        @block.scalar
        def _(act):
            act.wait_ge(S["w_cols"], 1)
            nc.scalar.copy(w_ext[:, :], ps_a[:, 0:F + 2 * HEADS]).then_inc(S["w_kept"], 1)
            for g in range(GROUPS):
                act.wait_ge(S["rstd_done"], 2 * g + 1)
                nc.scalar.activation(rstd[:, :], rstd[:, :], ACT.Sqrt).then_inc(S["sq"], 1)
                act.wait_ge(S["turned"], g + 1)
                nc.scalar.activation(h_T[:, :], ps_a[:, :], ACT.Relu).then_inc(S["relued"], 1)
                act.wait_ge(S["rows_kept"], g + 1)
                act.dma_start(table[g * PG * P:(g + 1) * PG * P, :].rearrange("(a p) f -> p a f", p=P),
                              rows[:, g % 2]).then_inc(S[f"rows_st{g % 2}"], 16)
            with act.Fori(0, T) as m:
                for c in range(CHUNKS):
                    act.wait_ge(S["dv"], (m * CHUNKS + c) * 2 + 2)
                    nc.scalar.activation(tau[:, :, :, :], tau[:, :, :, :], ACT.Exp).then_inc(S["exp_done"], 1)

        @block.vector
        def _(dve):
            nc.vector.memset(ones[:, :], 1.0)
            nc.vector.memset(att_block[:, :], 0.0).then_inc(S["w_turned"], 1)
            nc.vector.memset(rows[:, :, :, :], 1.0)
            dve.wait_ge(S["w_turned"], 1)
            dve.wait_ge(S["consts_in"], 80)
            for h in range(HEADS):
                for k in range(2):
                    last = nc.vector.tensor_copy(att_block[FO * h:FO * (h + 1), k * HEADS + h:k * HEADS + h + 1],
                                                 att_col[FO * h:FO * (h + 1), k:k + 1])
            last.then_inc(S["setup"], 1)
            for g in range(GROUPS):
                dve.wait_ge(S[f"x_in{g % 2}"], 16 * (g // 2 + 1))
                for a in range(PG):
                    last = nc.vector.bn_stats(stats[:, a, :], x_in[:, g % 2, a, :])
                last.then_inc(S["stats_done"], 1)
                dve.wait_ge(S["stats_done"], g + 1)
                for a in range(PG):
                    last = nc.vector.bn_aggr(moments[:, a, :], stats[:, a, :])
                last.then_inc(S["moments_done"], 1)
                dve.wait_ge(S["moments_done"], g + 1)
                nc.vector.tensor_scalar(rstd[:, :], moments[:, :, 1], EPS, None, ALU.add).then_inc(S["rstd_done"], 1)
                dve.wait_ge(S["sq"], g + 1)
                nc.vector.reciprocal(rstd[:, :], rstd[:, :]).then_inc(S["rstd_done"], 1)
                dve.wait_ge(S["rstd_done"], 2 * g + 2)
                if g >= 1:
                    dve.wait_ge(S["turned"], g)
                for a in range(PG):
                    last = nc.vector.tensor_scalar(x_norm[:, a, :], x_in[:, g % 2, a, :], moments[:, a, 0:1],
                                                   rstd[:, a:a + 1], ALU.subtract, ALU.mult)
                last.then_inc(S["normed"], 1)
                dve.wait_ge(S["projected"], g + 1)
                if g >= 2:
                    dve.wait_ge(S[f"rows_st{g % 2}"], 16 * (g // 2))
                for b in range(2):
                    pr = ps_b[:, b, 0:2 * 136].rearrange("p (a w) -> p a w", a=2)
                    nc.vector.tensor_copy(rows[:, g % 2, 2 * b:2 * b + 2, 0:VAL].rearrange("p a (h c) -> p a h c", h=HEADS)[:, :, :, 0:FO],
                                          pr[:, :, 0:F].rearrange("p a (h c) -> p a h c", h=HEADS))
                    nc.vector.tensor_copy(rows[:, g % 2, 2 * b:2 * b + 2, VAL:ROW], pr[:, :, F:F + HEADS])
                    last = nc.vector.tensor_copy(alpha_dst[:, g * PG + 2 * b:g * PG + 2 * b + 2, :], pr[:, :, F + HEADS:F + 2 * HEADS])
                last.then_inc(S["rows_kept"], 1)
            with dve.Fori(0, T) as m:
                dve.wait_ge(S["rows_kept"], GROUPS)
                dve.wait_ge(S["bc_done"], m)
                nc.vector.tensor_tensor(dst_diag[:, :, :], ident.unsqueeze(1).to_broadcast([P, HEADS, P]),
                                        alpha_dst[:, bass.ds(m, 1), :].rearrange("p a h -> p (a h)").unsqueeze(2).to_broadcast([P, HEADS, P]),
                                        ALU.mult).then_inc(S["diag_made"], 1)
                nc.vector.memset(acc[:, :], 0.0)
                dve.wait_ge(S["bc_done"], m + 1)
                nc.vector.tensor_copy(dst_bc[:, :, :].rearrange("p a b -> p (a b)"), ps_a[:, :]).then_inc(S["bc_kept"], 1)
                dve.wait_ge(S["bc_kept"], m + 1)
                for c in range(CHUNKS):
                    k = m * CHUNKS + c
                    dve.wait_ge(S[f"src_in{c % 2}"], m * (8 * CHUNKS) + 16 * (c // 2 + 1))
                    dve.wait_ge(S[f"adj_in{c % 2}"], m * (8 * CHUNKS) + 16 * (c // 2 + 1))
                    dve.wait_ge(S["mm_done"], k) if c else dve.wait_ge(S["mm_done"], m * CHUNKS)
                    nc.vector.tensor_tensor(tau[:, :, :, :], dst_bc[:, :, :].unsqueeze(1).to_broadcast([P, CH, HEADS, P]),
                                            src_rows[:, c % 2, :, VAL:ROW].unsqueeze(3).to_broadcast([P, CH, HEADS, P]),
                                            ALU.add).then_inc(S["dv"], 1)
                    dve.wait_ge(S["dv"], k * 2 + 1)
                    nc.vector.scalar_tensor_tensor(tau_flat, tau_flat, SLOPE, tau_flat, ALU.mult, ALU.max).then_inc(S["dv"], 1)
                    dve.wait_ge(S["exp_done"], k + 1)
                    nc.vector.tensor_tensor(tau[:, :, :, :], tau[:, :, :, :],
                                            adj_blk[:, c % 2].unsqueeze(2).to_broadcast([P, CH, HEADS, P]), ALU.mult).then_inc(S["tau_done"], 1)
                    dve.wait_ge(S["mm_done"], k + 1)
                    nc.vector.tensor_tensor(acc[:, :], acc[:, :], ps_c[:, 0:VAL], ALU.add).then_inc(S["acc_done"], 1)
                    dve.wait_ge(S["acc_done"], k + 1)
                av = acc[:, :].rearrange("p (h c) -> p h c", h=HEADS)
                nc.vector.reciprocal(rden[:, :], av[:, :, FO]).then_inc(S["turned"], 1)
                dve.wait_ge(S["turned"], m + (GROUPS + 1))
                dve.wait_ge(S["out_stored"], m * 16)
                zv = z_out[:, :].rearrange("p (h c) -> p h c", h=HEADS)
                nc.vector.tensor_tensor(zv, av[:, :, 0:FO], rden[:, :].unsqueeze(2).to_broadcast([P, HEADS, FO]), ALU.mult).then_inc(S["w_turned"], 1)
                dve.wait_ge(S["w_turned"], 2 * m + 2)
                nc.vector.tensor_tensor(z_out[:, :], z_out[:, :], bias_sb[:, :], ALU.add).then_inc(S["w_turned"], 1)
                dve.wait_ge(S["w_turned"], 2 * m + 3)
                dve.wait_ge(S["res_in"], m * 16 + 16)
                nc.vector.tensor_tensor(z_out[:, :], z_out[:, :], x_res[:, :], ALU.add).then_inc(S["fin_done"], 1)
                dve.wait_ge(S["fin_done"], m + 1)


def kernel(x, adj, L0_gnn_weight, L0_gnn_att_src, L0_gnn_att_dst, L0_gnn_bias):
    import numpy as np
    import concourse.bacc as bacc
    from concourse.bass_utils import run_bass_kernel_spmd

    nc = bacc.Bacc("TRN2", target_bir_lowering=False, num_devices=1)
    host = {"x": x, "adj": adj, "weight": L0_gnn_weight, "att_src": L0_gnn_att_src, "att_dst": L0_gnn_att_dst,
            "bias": L0_gnn_bias, "consts": np.eye(P, dtype=np.float32)}
    arrays, args = {}, []
    for name, a in host.items():
        a = np.ascontiguousarray(a)
        arrays[f"in_{name}"] = a
        args.append(nc.dram_tensor(f"in_{name}", a.shape, mybir.dt.from_np(a.dtype), kind="ExternalInput").ap())
    out = nc.dram_tensor("out", x.shape, F32, kind="ExternalOutput").ap()
    gat_kernel(nc, *args, out)
    return run_bass_kernel_spmd(nc, [arrays], core_ids=[0]).results[0]["out"]
```

```python
from contextlib import ExitStack

import concourse.bass as bass
from concourse import mybir

F32 = mybir.dt.float32
BF16 = mybir.dt.bfloat16
U16 = mybir.dt.uint16
U32 = mybir.dt.uint32
I32 = mybir.dt.int32
ALU = mybir.AluOpType
ACT = mybir.ActivationFunctionType
AX_X = mybir.AxisListType.X

P = 128
HEADS = 4
EPS = 1e-5
SLOPE = 0.2

PACK = 16
GPT = P // PACK
TOP = 8
SLOTS = 2 * TOP
BITS = 3
BLOCKS = 6
EDGES = BLOCKS * P
PAIR = 2
LEAST = 2.0 ** -126
BIAS_EXP = 127
MANTISSA = 23


class Steps:

    def __init__(self, sem, total, q):
        self.sem, self.total, self.base, self.n = sem, total, q * total, 0

    def mark(self, instruction):
        instruction.then_inc(self.sem, 1)
        self.n += 1
        return self.n

    def wait(self, engine, n=None):
        engine.wait_ge(self.sem, self.base + (self.n if n is None else n))


def const_layout(n_codes):
    widths = [("before", P), ("slot", SLOTS), ("edge_of", BLOCKS), ("pack", GPT)]
    at, cols = 0, {}
    for name, w in widths:
        cols[name] = (at, at + w)
        at += w
    return cols, at


def gat_kernel(nc, x, adj, weight, att_src, att_dst, bias, eye, consts, edges, masks, out, force_dense=False):
    N, F = x.shape
    T = N // P
    PAIRS = T // PAIR
    FO = F // HEADS
    HC = FO + 1
    VAL = HEADS * HC
    ROW = VAL + HEADS
    EXT = F + 2 * HEADS
    CODES = N // PACK
    PG = 4
    GROUPS = T // PG
    RING = 8
    CHUNKS = RING // PAIR
    CT = T // CHUNKS
    NB = PAIR * BLOCKS
    C_OFF = SLOTS
    C_DST = C_OFF + 1
    C_HOT = C_DST + HEADS
    LW = C_HOT + P
    DC = 8
    DCHUNKS = T // DC
    assert CODES == 512 and LW * 3 <= 512

    cols, n_const = const_layout(CODES)
    table = nc.dram_tensor("node_table", (N, ROW), F32, kind="Internal").ap()

    with ExitStack() as ctx:
        def sb(name, shape, dt=F32):
            return ctx.enter_context(nc.sbuf_tensor(name, shape, dt))

        def psum(name, shape, dt=F32):
            return ctx.enter_context(nc.psum_tensor(name, shape, dt))

        def sem(name):
            return ctx.enter_context(nc.semaphore(name))

        ring = sb("ring", [P, RING, CT, PAIR * P])
        x_all = sb("x_all", [P, T, F])
        const_sb = sb("const_sb", [P, n_const])
        edge_no_sb = sb("edge_no_sb", [P, EDGES], U16)
        edge_no = edge_no_sb[:, :]
        mask_sb = sb("mask_sb", [P, 2], U32)
        pack_w = sb("pack_w", [P, GPT], BF16)
        att_col = sb("att_col", [P, 2])
        alpha_dst = sb("alpha_dst", [P, T, HEADS])
        codes_left = sb("codes_left", [P, PAIR, CODES])
        top_code = sb("top_code", [P, PAIR, SLOTS])
        top_at = sb("top_at", [P, PAIR, SLOTS], U32)
        src_base = sb("src_base", [P, PAIR, SLOTS])
        bit = sb("bit", [P, BITS, PAIR, SLOTS])
        rest = sb("rest", [P, BITS, PAIR, SLOTS])
        bit_at = sb("bit_at", [P, BITS, PAIR, SLOTS], U32)
        cand_raw = sb("cand_raw", [P, BITS, PAIR, SLOTS])
        cand = sb("cand", [P, PAIR, BITS, SLOTS])
        cand_left = bit_at[:, :, :, :].rearrange("p k b s -> p (k b s)").bitcast(F32).rearrange(
            "p (b k s) -> p b k s", b=PAIR, k=BITS)
        is_src = sb("is_src", [P, PAIR, SLOTS])
        degree = sb("degree", [P, PAIR])
        lists = sb("lists", [P, 2, PAIR, LW])
        edge_end = sb("edge_end", [P, PAIR])
        over_slots = sb("over_slots", [P, PAIR])
        over_lists = sb("over_lists", [P, PAIR])
        least_degree = sb("least_degree", [P, PAIR])
        over_bits = sb("over_bits", [P, PAIR, SLOTS])
        over_edges = sb("over_edges", [P, PAIR])
        of_target = sb("of_target", [P, PAIR, EDGES])
        edge_rows = sb("edge_rows", [P, 2, NB, LW])
        place = sb("place", [P, NB])
        place_hot = sb("place_hot", [P, NB, SLOTS])
        src_next = sb("src_next", [P, NB])
        no_edge = sb("no_edge", [P, NB])
        is_edge = sb("is_edge", [P, 2, NB])
        src_idx = sb("src_idx", [P, 2, NB], U32)
        gathered = sb("gathered", [P, 2, NB, ROW])
        logit = sb("logit", [P, NB, HEADS])
        tau = sb("tau", [P, NB, HEADS])
        rden = sb("rden", [P, PAIR, HEADS])
        z_out = sb("z_out", [P, PAIR, F])
        over = sb("over", [P, 5])
        over_any = sb("over_any", [P, 1])
        flag = sb("flag", [P, 1], I32)

        stats = edge_rows[:, 0, 0:3, :].rearrange("p a b -> p (a b)")[:, 0:T * 6].rearrange("p (t s) -> p t s", s=6)
        moments = edge_rows[:, 0, 3, 0:2 * T].rearrange("p (t s) -> p t s", s=2)
        rstd = edge_rows[:, 0, 4, 0:T]
        var_eps = edge_rows[:, 0, 5, 0:T]
        rstd_sq = edge_rows[:, 0, 6, 0:T]
        x_norm = of_target[:, :, 0:PG * P].rearrange("p u (a f) -> p u a f", f=F)
        spare = edge_rows[:, 1].rearrange("p a b -> p (a b)")
        h_T = spare[:, 0:2 * PG * P].rearrange("p (u n) -> p u n", u=2)
        w_sb = spare[:, 1024:1024 + F]
        w_ext = spare[:, 1152:1152 + EXT]
        att_block = spare[:, 1288:1288 + 2 * HEADS]
        bias_sb = spare[:, 1296:1296 + F]
        ident = lists[:, 0, 0, C_HOT:LW]
        ones = of_target[:, 0, 0:P]
        table_rows = gathered[:, :, 0:PG, :]

        ring_flat = ring[:, :, :, :].rearrange("p a b c -> p (a b c)")
        at = [0]

        def carve(*shape):
            n = 1
            for s in shape:
                n *= s
            ap = ring_flat[:, at[0]:at[0] + n]
            at[0] += n
            names = "abcd"[:len(shape)]
            if len(shape) == 1:
                return ap
            return ap.rearrange(f"p ({' '.join(names)}) -> p {' '.join(names)}", **dict(zip(names, shape)))

        d_adj = carve(2, DC, P)
        d_src = carve(2, DC, ROW)
        d_diag = carve(HEADS, P)
        d_dst = carve(HEADS, P)
        d_tau = carve(DC, HEADS, P)
        d_tau_flat = d_tau.rearrange("p a b c -> p (a b c)")
        d_acc = carve(VAL)
        d_rden = carve(HEADS)
        d_z = carve(F)

        ps_codes = psum("ps_codes", [P, 2, PAIR, CODES])
        ps_edge = psum("ps_edge", [P, 2, 512])
        ps_sum = psum("ps_sum", [P, 512])
        ps_misc = psum("ps_misc", [P, 512])

        def edge_view(ap):
            return ap[:, :, 0:3 * LW].rearrange("p k (b c) -> p k b c", c=LW)

        names = """waits_held consts_in att_zeroed att_ready pack_ready ones_ready projection_ready projection_kept
            moments_ready root_ready root_done rstd_ready normed turned relued projected rows_kept rows_in0 rows_in1
            gather_zeroed over_zeroed
            ring_free packed codes_free decode degree_ready offset_done lists_done
            first_found of_target_ready edges_spread edges_kept
            place_steps idx_ready idx_used gathered0 gathered1 logit_added logit_ready tau_ready tau_masked weighted summed
            rden_ready z_scaled z_ready z_stored
            over_ready over_summed flag_ready
            d_adj0 d_adj1 d_src0 d_src1 d_diag_ready d_dst_done d_dst_kept d_logit d_exp d_tau_ready d_product d_added
            d_rden_ready d_z_scaled d_z_ready d_z_stored d_z_free""".split()
        S = {n: sem(n) for n in names}
        ring_in = [sem(f"ring_in{k}") for k in range(RING)]
        ring_used = [sem(f"ring_used{k}") for k in range(RING)]
        N_CONST_DMAS = 13

        block = ctx.enter_context(nc.Block())
        before = const_sb[:, cols["before"][0]:cols["before"][1]]
        slot_no = const_sb[:, cols["slot"][0]:cols["slot"][1]]
        edge_of = const_sb[:, cols["edge_of"][0]:cols["edge_of"][1]]
        pack_f = const_sb[:, cols["pack"][0]:cols["pack"][1]]

        def lagged(i, u, lag):
            n = u - lag
            return i + n // 2, n % 2

        def waited(engine):
            engine.sem_inc(S["waits_held"], 1)

        def slots(engine, slot, first, last, even_from, even_to):
            for s in range(first, even_from):
                slot(s // 2, s % 2, s)
            with engine.Fori(even_from // 2, even_to // 2) as i:
                for u in range(2):
                    slot(i, u, None)
            for s in range(even_to, last):
                slot(s // 2, s % 2, s)

        @block.sync
        def _(sp):
            for u in range(2):
                for b in range(PAIR):
                    sp.dma_start(lists[:, u, b, C_HOT:LW], eye).then_inc(S["consts_in"], 16)
            sp.dma_start(const_sb[:, :], consts).then_inc(S["consts_in"], 16)
            sp.dma_start(edge_no, edges).then_inc(S["consts_in"], 16)
            sp.dma_start(mask_sb[:, :], masks).then_inc(S["consts_in"], 16)
            sp.dma_start(w_sb, weight).then_inc(S["consts_in"], 16)
            sp.dma_start(att_col[:, 0:1], att_src.rearrange("a h f -> (h f) a")).then_inc(S["consts_in"], 16)
            sp.dma_start(att_col[:, 1:2], att_dst.rearrange("a h f -> (h f) a")).then_inc(S["consts_in"], 16)
            sp.dma_start(bias_sb, bias.rearrange("(a f) -> a f", a=1).to_broadcast([P, F])
                         ).then_inc(S["consts_in"], 16)
            for half in range(2):
                rows = slice(half * T // 2, (half + 1) * T // 2)
                sp.dma_start(x_all[:, rows, :], x.rearrange("(t p) f -> p t f", p=P)[:, rows, :]
                             ).then_inc(S["consts_in"], 16)
            with sp.Fori(0, PAIRS // 2) as i:
                for k in range(RING):
                    u, c = k // CHUNKS, k % CHUNKS
                    sp.wait_ge(ring_used[k], i + 1)
                    sp.dma_start(ring[:, k], adj[c * CT * P:(c + 1) * CT * P, bass.ds((2 * i + u) * PAIR * P, PAIR * P)]
                                 .rearrange("(t p) m -> p t m", p=P)).then_inc(ring_in[k], 16)
            sp.wait_ge(S["z_stored"], 16 * PAIRS)
            sp.wait_ge(S["flag_ready"], 1)
            with sp.If(sp.value_load(flag[0:1, 0:1], min_val=0, max_val=P * 5) > 0):
                with sp.Fori(0, T) as m:
                    for c in range(DCHUNKS):
                        sp.wait_ge(S["d_product"], m * DCHUNKS + (c if c > 1 else 1))
                        sp.dma_start(d_adj[:, c % 2], adj[c * DC * P:(c + 1) * DC * P, bass.ds(m * P, P)]
                                     .rearrange("(t p) m -> p t m", p=P)).then_inc(S[f"d_adj{c % 2}"], 16)
                        sp.dma_start(d_src[:, c % 2], table[c * DC * P:(c + 1) * DC * P, :]
                                     .rearrange("(t p) c -> p t c", p=P)).then_inc(S[f"d_src{c % 2}"], 16)
                    sp.wait_ge(S["d_z_ready"], m + 1)
                    sp.dma_start(out[bass.ds(m * P, P), :], d_z).then_inc(S["d_z_stored"], 16)
                    sp.wait_ge(S["d_z_stored"], m * 16 + 16)
                    sp.sem_inc(S["d_z_free"], 1)

        @block.gpsimd
        def _(pool):
            for k in range(RING):
                pool.sem_inc(ring_used[k], 1)
            pool.wait_ge(S["normed"], GROUPS)
            nc.gpsimd.tensor_tensor(x_all[:, :, :], x_all[:, :, :],
                                    bias_sb.unsqueeze(1).to_broadcast([P, T, F]), ALU.add
                                    ).then_inc(S["gather_zeroed"], 1)
            pool.wait_ge(S["rows_in0"], 16 * GROUPS // 2)
            pool.wait_ge(S["rows_in1"], 16 * GROUPS // 2)
            nc.gpsimd.memset(gathered[:, :, :, :], 0.0).then_inc(S["gather_zeroed"], 1)
            pool.wait_ge(S["gather_zeroed"], 2)
            with pool.Fori(0, PAIRS // 2) as i:
                for u in range(2):
                    q = 2 * i + u
                    pool.wait_ge(S["idx_ready"], q + 1)
                    pool.wait_ge(S["summed"], q + 1)
                    waited(pool)
                    for b in range(NB):
                        pool.indirect_dma_start(gathered[:, u, b, :], None, table[:, :],
                                                bass.IndirectOffsetOnAxis(src_idx[:, u, b:b + 1], 0),
                                                bounds_check=N - 1, oob_is_err=False
                                                ).then_inc(S[f"gathered{u}"], 16)

        @block.tensor
        def _(pe):
            pe.sem_inc(S["summed"], 2)
            pe.sem_inc(S["d_product"], 1)
            pe.wait_ge(S["consts_in"], 16 * N_CONST_DMAS)
            pe.wait_ge(S["att_ready"], 1)
            pe.transpose(ps_misc[:, 0:F], w_sb, ident)
            pe.matmul(ps_misc[:, F:EXT], w_sb, att_block, start=True, stop=True
                      ).then_inc(S["projection_ready"], 1)

            turned_at = [ps_sum, ps_misc]

            def turn(g, u):
                pe.wait_ge(S["normed"], g + 1)
                pe.wait_ge(S["relued"], g + 1)
                for a in range(PG):
                    last = pe.transpose(turned_at[u][:, a * P:(a + 1) * P], x_norm[:, u, a, :], ident)
                last.then_inc(S["turned"], 1)

            def project(g, u):
                pe.wait_ge(S["relued"], g + 3)
                pe.wait_ge(S["rows_kept"], g + 1)
                for a in range(PG):
                    last = pe.matmul(ps_edge[:, a // 2, (a % 2) * EXT:(a % 2 + 1) * EXT], h_T[:, u, a * P:(a + 1) * P],
                                     w_ext, start=True, stop=True)
                last.then_inc(S["projected"], 1)

            pe.wait_ge(S["projection_kept"], 1)
            turn(0, 0)
            with pe.Fori(0, GROUPS // 2 - 1) as i:
                turn(2 * i + 1, 1)
                project(2 * i, 0)
                turn(2 * i + 2, 0)
                project(2 * i + 1, 1)
            turn(GROUPS - 1, 1)
            project(GROUPS - 2, 0)
            project(GROUPS - 1, 1)
            pe.wait_ge(S["rows_kept"], GROUPS + 1)

            def pack(i, u, c):
                q = 2 * i + u
                if c == 0:
                    pe.wait_ge(S["codes_free"], q + 1)
                k = u * CHUNKS + c
                pe.wait_ge(ring_in[k], 16 * i + 16)
                halves = ring[:, k].rearrange("p t m -> p (t m)").bitcast(BF16).rearrange(
                    "p (t b m e) -> p t b m e", b=PAIR, m=P, e=2)
                for b in range(PAIR):
                    for t in range(CT):
                        at_code = (c * CT + t) * GPT
                        last = pe.matmul(ps_codes[:, u, b, at_code:at_code + GPT], halves[:, t, b, :, 1],
                                         pack_w[:, :], start=True, stop=True)
                last.then_inc(ring_used[k], 1)

            def offsets(i, u):
                q = 2 * i + u
                pe.wait_ge(S["degree_ready"], q + 1)
                pe.wait_ge(S["lists_done"], q + 1)
                pe.matmul(ps_misc[:, 0:PAIR], before, degree[:, :], start=True, stop=True
                          ).then_inc(S["offset_done"], 1)

            def spread(i, u):
                q = 2 * i + u
                for b in range(PAIR):
                    pe.wait_ge(S["of_target_ready"], 2 * q + (b + 1))
                    pe.wait_ge(S["edges_kept"], 2 * q + (b + 1))
                    for e in range(BLOCKS):
                        last = pe.matmul(ps_edge[:, e // 3, (e % 3) * LW:(e % 3 + 1) * LW],
                                         of_target[:, b, e * P:(e + 1) * P], lists[:, u, b, :], start=True, stop=True)
                    last.then_inc(S["edges_spread"], 1)

            def sum_edges(i, u):
                q = 2 * i + u
                pe.wait_ge(S["weighted"], q + 1)
                pe.wait_ge(S["z_scaled"], q + 1)
                for b in range(PAIR):
                    for e in range(BLOCKS):
                        n = b * BLOCKS + e
                        last = pe.matmul(ps_sum[:, b * VAL:(b + 1) * VAL], edge_rows[:, u, n, C_HOT:LW],
                                         gathered[:, u, n, 0:VAL], start=(e == 0), stop=(e == BLOCKS - 1))
                last.then_inc(S["summed"], 1)

            for c in range(CHUNKS):
                pack(0, 0, c)

            def slot(i, u, s):
                nxt, three = lagged(i, u, -1), lagged(i, u, 2)
                more, body, back = (s is None or s + 1 < PAIRS), (s is None or s < PAIRS), (s is None or s >= 2)
                for c in range(CHUNKS):
                    if more:
                        pack(*nxt, c)
                    if c == 1 and body:
                        offsets(i, u)
                    if c == 2 and back:
                        sum_edges(*three)
                if body:
                    spread(i, u)

            slots(pe, slot, 0, PAIRS + 2, 2, PAIRS - 2)

            pe.wait_ge(S["over_ready"], 1)
            pe.wait_ge(S["ones_ready"], 1)
            pe.matmul(ps_misc[:, 0:5], ones, over[:, :], start=True, stop=True).then_inc(S["over_summed"], 1)

            pe.wait_ge(S["flag_ready"], 1)
            with pe.If(pe.value_load(flag[0:1, 0:1], min_val=0, max_val=P * 5) > 0):
                with pe.Fori(0, T) as m:
                    pe.wait_ge(S["d_diag_ready"], m + 1)
                    pe.matmul(ps_misc[:, :], ones, d_diag.rearrange("p h m -> p (h m)"), start=True, stop=True
                              ).then_inc(S["d_dst_done"], 1)
                    for c in range(DCHUNKS):
                        k = m * DCHUNKS + c
                        pe.wait_ge(S["d_tau_ready"], k + 1)
                        pe.wait_ge(S["d_added"], k + 1)
                        for h in range(HEADS):
                            for t in range(DC):
                                last = pe.matmul(ps_sum[:, h * HC:(h + 1) * HC], d_tau[:, t, h, :],
                                                 d_src[:, c % 2, t, h * HC:(h + 1) * HC],
                                                 start=(t == 0), stop=(t == DC - 1))
                        last.then_inc(S["d_product"], 1)

        @block.scalar
        def _(act):
            act.sem_inc(S["relued"], 2)
            act.sem_inc(S["edges_kept"], 1)
            act.wait_ge(S["projection_ready"], 1)
            nc.scalar.copy(w_ext, ps_misc[:, 0:EXT]).then_inc(S["projection_kept"], 1)
            act.wait_ge(S["root_ready"], 1)
            nc.scalar.activation(rstd, var_eps, ACT.Sqrt).then_inc(S["root_done"], 1)
            turned_at = [ps_sum, ps_misc]
            with act.Fori(0, GROUPS // 2) as i:
                for u in range(2):
                    g = 2 * i + u
                    act.wait_ge(S["turned"], g + 1)
                    act.wait_ge(S["projected"], g + 1)
                    nc.scalar.activation(h_T[:, u, :], turned_at[u][:, :], ACT.Relu).then_inc(S["relued"], 1)
                    act.wait_ge(S["rows_kept"], g + 2)
                    act.dma_start(table[bass.ds(g * PG * P, PG * P), :].rearrange("(a p) c -> p a c", p=P),
                                  table_rows[:, u]).then_inc(S[f"rows_in{u}"], 16)
            act.wait_ge(S["gather_zeroed"], 2)

            def keep_edges(i, u):
                q = 2 * i + u
                act.wait_ge(S["summed"], q + 1)
                for b in range(PAIR):
                    act.wait_ge(S["edges_spread"], 2 * q + (b + 1))
                    nc.scalar.copy(edge_rows[:, u, b * BLOCKS:(b + 1) * BLOCKS, :].rearrange("p (k b) c -> p k b c", k=2),
                                   edge_view(ps_edge)).then_inc(S["edges_kept"], 1)

            def exponentials(i, u):
                q = 2 * i + u
                act.wait_ge(S["logit_ready"], q + 1)
                nc.scalar.activation(tau[:, :, :], logit[:, :, :], ACT.Exp).then_inc(S["tau_ready"], 1)

            def store(i, u):
                q = 2 * i + u
                act.wait_ge(S["z_ready"], q + 1)
                act.dma_start(out[bass.ds(q * PAIR * P, PAIR * P), :].rearrange("(b p) f -> p b f", p=P)
                              if not isinstance(q, int) else
                              out[q * PAIR * P:(q + 1) * PAIR * P, :].rearrange("(b p) f -> p b f", p=P),
                              z_out[:, :, :]).then_inc(S["z_stored"], 16)

            def slot(i, u, s):
                if s is None or 2 <= s < PAIRS + 2:
                    exponentials(*lagged(i, u, 2))
                if s is None or s < PAIRS:
                    keep_edges(i, u)
                if s is None or s >= 3:
                    store(*lagged(i, u, 3))

            slots(act, slot, 0, PAIRS + 3, 4, PAIRS)

            act.wait_ge(S["flag_ready"], 1)
            with act.If(act.value_load(flag[0:1, 0:1], min_val=0, max_val=P * 5) > 0):
                with act.Fori(0, T) as m:
                    for c in range(DCHUNKS):
                        act.wait_ge(S["d_logit"], 2 * (m * DCHUNKS + c) + 2)
                        nc.scalar.activation(d_tau_flat, d_tau_flat, ACT.Exp).then_inc(S["d_exp"], 1)

        @block.vector
        def _(dve):
            dve.sem_inc(S["rows_kept"], 1)
            dve.sem_inc(S["projected"], 2)
            dve.sem_inc(S["codes_free"], 2)
            dve.sem_inc(S["lists_done"], 1)
            dve.sem_inc(S["z_scaled"], 1)
            dve.sem_inc(S["d_added"], 1)
            dve.sem_inc(S["d_z_free"], 1)
            v = nc.vector
            v.memset(att_block, 0.0).then_inc(S["att_zeroed"], 1)
            dve.wait_ge(S["att_zeroed"], 1)
            dve.wait_ge(S["consts_in"], 16 * N_CONST_DMAS)
            for h in range(HEADS):
                for k in range(2):
                    last = v.tensor_copy(att_block[FO * h:FO * (h + 1), k * HEADS + h:k * HEADS + h + 1],
                                         att_col[FO * h:FO * (h + 1), k:k + 1])
            last.then_inc(S["att_ready"], 1)
            v.tensor_copy(pack_w[:, :], pack_f)
            v.memset(over[:, :], 0.0)
            v.memset(over_slots[:, :], 0.0)
            v.memset(over_lists[:, :], 0.0)
            v.memset(least_degree[:, :], 1.0)
            v.memset(over_bits[:, :, :], 0.0)
            v.memset(over_edges[:, :], 0.0).then_inc(S["over_zeroed"], 1)
            for t in range(T):
                last = v.bn_stats(stats[:, t, :], x_all[:, t, :])
            last.then_inc(S["moments_ready"], 1)
            dve.wait_ge(S["moments_ready"], 1)
            for t in range(T):
                last = v.bn_aggr(moments[:, t, :], stats[:, t, :])
            last.then_inc(S["moments_ready"], 1)
            dve.wait_ge(S["moments_ready"], 2)
            v.tensor_scalar(var_eps, moments[:, :, 1], EPS, None, ALU.add).then_inc(S["root_ready"], 1)
            dve.wait_ge(S["root_done"], 1)
            r = Steps(S["rstd_ready"], 5, 0)
            r.mark(v.reciprocal(rstd, rstd))
            r.wait(dve)
            r.mark(v.tensor_tensor(rstd_sq, rstd, rstd, ALU.mult))
            r.wait(dve)
            r.mark(v.tensor_tensor(rstd_sq, rstd_sq, var_eps, ALU.mult))
            r.wait(dve)
            r.mark(v.tensor_scalar(rstd_sq, rstd_sq, -0.5, 1.5, ALU.mult, ALU.add))
            r.wait(dve)
            r.mark(v.tensor_tensor(rstd, rstd, rstd_sq, ALU.mult))
            r.wait(dve)
            v.memset(table_rows, 1.0)

            def normalise(g, u):
                for a in range(PG):
                    t = g * PG + a
                    one = (lambda ap: ap[:, bass.ds(t, 1)]) if not isinstance(t, int) else (lambda ap: ap[:, t:t + 1])
                    last = v.tensor_scalar(x_norm[:, u, a, :], one(x_all[:, :, :]).rearrange("p a f -> p (a f)"),
                                           one(moments[:, :, 0]), one(rstd), ALU.subtract, ALU.mult)
                last.then_inc(S["normed"], 1)

            def keep_rows(g, u):
                for k in range(2):
                    got = ps_edge[:, k, 0:2 * EXT].rearrange("p (a c) -> p a c", c=EXT)
                    rows = table_rows[:, u, 2 * k:2 * k + 2, :]
                    v.tensor_copy(rows[:, :, 0:VAL].rearrange("p a (h c) -> p a h c", c=HC)[:, :, :, 0:FO],
                                  got[:, :, 0:F].rearrange("p a (h c) -> p a h c", c=FO))
                    v.tensor_copy(rows[:, :, VAL:ROW], got[:, :, F:F + HEADS])
                    at_tile = g * PG + 2 * k
                    dst = alpha_dst[:, bass.ds(at_tile, 2), :] if not isinstance(g, int) else alpha_dst[:, at_tile:at_tile + 2, :]
                    last = v.tensor_copy(dst, got[:, :, F + HEADS:EXT])
                last.then_inc(S["rows_kept"], 1)

            for g in range(2):
                normalise(g, g)
            for g in range(GROUPS):
                u = g % 2
                dve.wait_ge(S["projected"], g + 3)
                if g >= 2:
                    dve.wait_ge(S[f"rows_in{u}"], 16 * (g // 2))
                keep_rows(g, u)
                if g + 2 < GROUPS:
                    normalise(g + 2, u)
            dve.wait_ge(S["over_zeroed"], 1)

            E_STEPS = 25

            def extract(i, u):
                q = 2 * i + u
                st = Steps(S["decode"], E_STEPS, q)
                for k in range(CHUNKS):
                    dve.wait_ge(ring_used[u * CHUNKS + k], i + 2)
                dve.wait_ge(S["edges_spread"], 2 * q - 2) if not isinstance(q, int) or q >= 2 else None
                both = range(PAIR)
                codes = [ps_codes[:, u, b, :] for b in both]
                first = [top_code[:, b, 0:TOP] for b in both]
                second = [top_code[:, b, TOP:SLOTS] for b in both]
                waited(dve)
                for b in both:
                    st.mark(v.max(first[b], codes[b]))
                st.wait(dve)
                waited(dve)
                for b in both:
                    st.mark(v.max_index(top_at[:, b, 0:TOP], first[b], codes[b]))
                for b in both:
                    last = v.match_replace(codes_left[:, b, :], first[b], codes[b], 0.0)
                last.then_inc(S["codes_free"], 1)
                dve.wait_ge(S["codes_free"], q + 3)
                waited(dve)
                for b in both:
                    st.mark(v.max(second[b], codes_left[:, b, :]))
                st.wait(dve)
                waited(dve)
                for b in both:
                    st.mark(v.max_index(top_at[:, b, TOP:SLOTS], second[b], codes_left[:, b, :]))
                mask = mask_sb[:, 0:1].unsqueeze(2).to_broadcast([P, PAIR, SLOTS])
                shift = mask_sb[:, 1:2].unsqueeze(2).unsqueeze(3).to_broadcast([P, BITS, PAIR, SLOTS])
                left = top_code[:, :, :]
                for k in range(BITS):
                    st.mark(v.tensor_tensor(bit[:, k].bitcast(U32), left.bitcast(U32), mask, ALU.bitwise_and))
                    if k == 1:
                        st.mark(v.tensor_scalar(src_base[:, :, :], top_at[:, :, :], float(PACK), float(1 - BIAS_EXP),
                                                ALU.mult, ALU.add))
                        st.wait(dve, st.n - 1)
                    else:
                        st.wait(dve)
                    st.mark(v.tensor_tensor(rest[:, k], left, bit[:, k], ALU.subtract))
                    if k < BITS - 1:
                        st.wait(dve)
                    left = rest[:, k]
                st.mark(v.tensor_tensor(bit_at[:, :, :, :].rearrange("p k b s -> p (k b s)"),
                                        bit[:, :, :, :].rearrange("p k b s -> p (k b s)").bitcast(U32),
                                        mask_sb[:, 1:2].to_broadcast([P, BITS * PAIR * SLOTS]), ALU.logical_shift_right))
                st.wait(dve)
                st.mark(v.tensor_tensor(cand_raw[:, :, :, :].rearrange("p k b s -> p k (b s)"),
                                        bit_at[:, :, :, :].rearrange("p k b s -> p k (b s)"),
                                        src_base[:, :, :].rearrange("p b s -> p (b s)").unsqueeze(1)
                                        .to_broadcast([P, BITS, PAIR * SLOTS]), ALU.add))
                st.wait(dve)
                for b in range(PAIR):
                    st.mark(v.scalar_tensor_tensor(cand[:, b], bit[:, :, b, :], 0.0, cand_raw[:, :, b, :],
                                                   ALU.is_gt, ALU.mult))
                st.wait(dve)
                waited(dve)
                flat = [cand[:, b].rearrange("p k s -> p (k s)") for b in both]
                flat_left = [cand_left[:, b].rearrange("p k s -> p (k s)") for b in both]
                for b in both:
                    st.mark(v.max(lists[:, u, b, 0:TOP], flat[b]))
                st.wait(dve)
                waited(dve)
                for b in both:
                    st.mark(v.match_replace(flat_left[b], lists[:, u, b, 0:TOP], flat[b], 0.0))
                st.wait(dve)
                waited(dve)
                for b in both:
                    st.mark(v.max(lists[:, u, b, TOP:SLOTS], flat_left[b]))
                st.wait(dve)
                assert st.n == E_STEPS, st.n
                v.tensor_scalar(is_src[:, :, :], lists[:, u, :, 0:SLOTS], 0.0, None, ALU.is_gt).then_inc(S["first_found"], 1)
                dve.wait_ge(S["first_found"], 3 * q + 1)
                v.tensor_reduce(degree[:, :], is_src[:, :, :], AX_X, ALU.add).then_inc(S["degree_ready"], 1)
                dve.wait_ge(S["degree_ready"], q + 1)
                v.tensor_tensor(over_slots[:, :], over_slots[:, :], top_code[:, :, SLOTS - 1], ALU.max)
                v.tensor_tensor(least_degree[:, :], least_degree[:, :], degree[:, :], ALU.min)
                v.tensor_tensor(over_bits[:, :, :], over_bits[:, :, :], rest[:, BITS - 1], ALU.max)

            def list_edges(i, u):
                q = 2 * i + u
                dve.wait_ge(S["offset_done"], q + 1)
                v.tensor_copy(lists[:, u, :, C_OFF], ps_misc[:, 0:PAIR])
                v.tensor_tensor(edge_end[:, :], ps_misc[:, 0:PAIR], degree[:, :], ALU.add).then_inc(S["lists_done"], 1)
                at_tile = q * PAIR
                d = alpha_dst[:, bass.ds(at_tile, PAIR), :] if not isinstance(q, int) else alpha_dst[:, at_tile:at_tile + PAIR, :]
                v.tensor_copy(lists[:, u, :, C_DST:C_DST + HEADS], d)
                v.tensor_tensor(over_lists[:, :], over_lists[:, :], lists[:, u, :, SLOTS - 1], ALU.max)
                dve.wait_ge(S["lists_done"], q + 2)
                if not isinstance(q, int) or q >= 1:
                    dve.wait_ge(S["edges_spread"], 2 * q)
                v.tensor_tensor(over_edges[:, :], over_edges[:, :], edge_end[:, :], ALU.max)
                for b in range(PAIR):
                    v.tensor_scalar(of_target[:, b, :], edge_no, lists[:, u, b, C_OFF:C_OFF + 1], None, ALU.is_ge
                                    ).then_inc(S["first_found"], 1)
                    dve.wait_ge(S["first_found"], 3 * q + (b + 2))
                    v.scalar_tensor_tensor(of_target[:, b, :], edge_no, edge_end[:, b:b + 1], of_target[:, b, :],
                                           ALU.is_lt, ALU.mult).then_inc(S["of_target_ready"], 1)
                    dve.wait_ge(S["of_target_ready"], 2 * q + (b + 1))

            def pick_sources(i, u):
                q = 2 * i + u
                st = Steps(S["place_steps"], 5, q)
                dve.wait_ge(S["edges_kept"], 2 * q + 3)
                if not isinstance(q, int) or q >= 2:
                    dve.wait_ge(S[f"gathered{u}"], i * (16 * NB))
                got = edge_rows[:, u]
                st.mark(v.tensor_tensor(place[:, :].rearrange("p (b e) -> p b e", b=PAIR),
                                        edge_of.unsqueeze(1).to_broadcast([P, PAIR, BLOCKS]),
                                        got[:, :, C_OFF].rearrange("p (b e) -> p b e", b=PAIR), ALU.subtract))
                st.wait(dve)
                st.mark(v.tensor_tensor(place_hot[:, :, :], slot_no.unsqueeze(1).to_broadcast([P, NB, SLOTS]),
                                        place[:, :].unsqueeze(2).to_broadcast([P, NB, SLOTS]), ALU.is_equal))
                st.wait(dve)
                st.mark(v.tensor_tensor(place_hot[:, :, :], place_hot[:, :, :], got[:, :, 0:SLOTS], ALU.mult))
                st.wait(dve)
                st.mark(v.tensor_reduce(src_next[:, :], place_hot[:, :, :], AX_X, ALU.add))
                st.wait(dve)
                st.mark(v.tensor_scalar(no_edge[:, :], src_next[:, :], 0.5, float(2 * N), ALU.is_lt, ALU.mult))
                v.tensor_scalar(is_edge[:, u, :], src_next[:, :], 0.5, None, ALU.is_gt)
                st.wait(dve)
                v.scalar_tensor_tensor(src_idx[:, u, :], src_next[:, :], -1.0, no_edge[:, :], ALU.add, ALU.add
                                       ).then_inc(S["idx_ready"], 1)

            def logits(i, u):
                q = 2 * i + u
                dve.wait_ge(S[f"gathered{u}"], i * (16 * NB) + 16 * NB)
                v.tensor_tensor(logit[:, :, :], gathered[:, u, :, VAL:ROW], edge_rows[:, u, :, C_DST:C_DST + HEADS],
                                ALU.add).then_inc(S["logit_added"], 1)
                dve.wait_ge(S["logit_added"], q + 1)
                v.scalar_tensor_tensor(logit[:, :, :], logit[:, :, :], SLOPE, logit[:, :, :], ALU.mult, ALU.max
                                       ).then_inc(S["logit_ready"], 1)

            def weigh(i, u):
                q = 2 * i + u
                dve.wait_ge(S["tau_ready"], q + 1)
                v.tensor_tensor(tau[:, :, :], tau[:, :, :], is_edge[:, u, :].unsqueeze(2).to_broadcast([P, NB, HEADS]),
                                ALU.mult).then_inc(S["tau_masked"], 1)
                dve.wait_ge(S["tau_masked"], q + 1)
                rows = gathered[:, u, :, 0:VAL].rearrange("p e (h c) -> p e h c", c=HC)
                v.tensor_tensor(rows, rows, tau[:, :, :].unsqueeze(3).to_broadcast([P, NB, HEADS, HC]), ALU.mult
                                ).then_inc(S["weighted"], 1)

            def finish(i, u):
                q = 2 * i + u
                dve.wait_ge(S["summed"], q + 3)
                sums = ps_sum[:, 0:PAIR * VAL].rearrange("p (b h c) -> p b h c", b=PAIR, c=HC)
                v.tensor_scalar(rden[:, :, :], sums[:, :, :, FO], LEAST, None, ALU.max).then_inc(S["rden_ready"], 1)
                dve.wait_ge(S["rden_ready"], 2 * q + 1)
                v.reciprocal(rden[:, :, :], rden[:, :, :]).then_inc(S["rden_ready"], 1)
                if not isinstance(q, int) or q >= 1:
                    dve.wait_ge(S["z_stored"], q * 16)
                dve.wait_ge(S["rden_ready"], 2 * q + 2)
                v.tensor_tensor(z_out[:, :, :].rearrange("p b (h c) -> p b h c", c=FO), sums[:, :, :, 0:FO],
                                rden[:, :, :].unsqueeze(3).to_broadcast([P, PAIR, HEADS, FO]), ALU.mult
                                ).then_inc(S["z_scaled"], 1)
                dve.wait_ge(S["z_scaled"], q + 2)
                at_tile = q * PAIR
                xs = x_all[:, bass.ds(at_tile, PAIR), :] if not isinstance(q, int) else x_all[:, at_tile:at_tile + PAIR, :]
                v.tensor_tensor(z_out[:, :, :], z_out[:, :, :], xs, ALU.add).then_inc(S["z_ready"], 1)

            def slot(i, u, s):
                if s is None or s < PAIRS:
                    extract(i, u)
                if s is None or 1 <= s < PAIRS + 1:
                    pick_sources(*lagged(i, u, 1))
                if s is None or 2 <= s < PAIRS + 2:
                    logits(*lagged(i, u, 2))
                if s is None or s < PAIRS:
                    list_edges(i, u)
                if s is None or 2 <= s < PAIRS + 2:
                    weigh(*lagged(i, u, 2))
                if s is None or s >= 3:
                    finish(*lagged(i, u, 3))

            dve.wait_ge(S["gather_zeroed"], 2)
            slots(dve, slot, 0, PAIRS + 3, 4, PAIRS)

            v.tensor_reduce(over[:, 0:1], over_slots[:, :], AX_X, ALU.max)
            v.tensor_reduce(over[:, 1:2], over_bits[:, :, :].rearrange("p b s -> p (b s)"), AX_X, ALU.max)
            v.tensor_reduce(over[:, 2:3], over_lists[:, :], AX_X, ALU.max)
            v.tensor_reduce(over[:, 3:4], over_edges[:, :], AX_X, ALU.max)
            v.tensor_reduce(over[:, 4:5], least_degree[:, :], AX_X, ALU.min).then_inc(S["over_zeroed"], 1)
            v.memset(ones, 1.0).then_inc(S["ones_ready"], 1)
            dve.wait_ge(S["over_zeroed"], 2)
            v.tensor_scalar(over[:, 0:3], over[:, 0:3], 0.0, None, ALU.is_gt)
            v.tensor_scalar(over[:, 4:5], over[:, 4:5], 0.5, None, ALU.is_lt)
            v.tensor_scalar(over[:, 3:4], over[:, 3:4], float(EDGES if not force_dense else 0), None, ALU.is_gt
                            ).then_inc(S["over_ready"], 1)
            dve.wait_ge(S["over_summed"], 1)
            v.tensor_reduce(over_any[:, :], ps_misc[:, 0:5], AX_X, ALU.add).then_inc(S["over_zeroed"], 1)
            dve.wait_ge(S["over_zeroed"], 3)
            v.tensor_copy(flag[:, :], over_any[:, :]).then_inc(S["flag_ready"], 1)
            dve.wait_ge(S["flag_ready"], 1)
            with dve.If(dve.value_load(flag[0:1, 0:1], min_val=0, max_val=P * 5) > 0):
                with dve.Fori(0, T) as m:
                    v.tensor_tensor(d_diag, ident.unsqueeze(1).to_broadcast([P, HEADS, P]),
                                    alpha_dst[:, bass.ds(m, 1), :].rearrange("p a h -> p (a h)").unsqueeze(2)
                                    .to_broadcast([P, HEADS, P]), ALU.mult).then_inc(S["d_diag_ready"], 1)
                    v.memset(d_acc, 0.0)
                    dve.wait_ge(S["d_dst_done"], m + 1)
                    v.tensor_copy(d_dst.rearrange("p h m -> p (h m)"), ps_misc[:, :]).then_inc(S["d_dst_kept"], 1)
                    dve.wait_ge(S["d_dst_kept"], m + 1)
                    for c in range(DCHUNKS):
                        k = m * DCHUNKS + c
                        dve.wait_ge(S[f"d_adj{c % 2}"], m * (8 * DCHUNKS) + 16 * (c // 2 + 1))
                        dve.wait_ge(S[f"d_src{c % 2}"], m * (8 * DCHUNKS) + 16 * (c // 2 + 1))
                        v.tensor_tensor(d_tau, d_dst.unsqueeze(1).to_broadcast([P, DC, HEADS, P]),
                                        d_src[:, c % 2, :, VAL:ROW].unsqueeze(3).to_broadcast([P, DC, HEADS, P]), ALU.add
                                        ).then_inc(S["d_logit"], 1)
                        dve.wait_ge(S["d_logit"], 2 * k + 1)
                        v.scalar_tensor_tensor(d_tau_flat, d_tau_flat, SLOPE, d_tau_flat, ALU.mult, ALU.max
                                               ).then_inc(S["d_logit"], 1)
                        dve.wait_ge(S["d_exp"], k + 1)
                        v.tensor_tensor(d_tau, d_tau, d_adj[:, c % 2].unsqueeze(2).to_broadcast([P, DC, HEADS, P]), ALU.mult
                                        ).then_inc(S["d_tau_ready"], 1)
                        dve.wait_ge(S["d_product"], k + 2)
                        v.tensor_tensor(d_acc, d_acc, ps_sum[:, 0:VAL], ALU.add).then_inc(S["d_added"], 1)
                        dve.wait_ge(S["d_added"], k + 2)
                    acc = d_acc.rearrange("p (h c) -> p h c", c=HC)
                    v.reciprocal(d_rden, acc[:, :, FO]).then_inc(S["d_rden_ready"], 1)
                    dve.wait_ge(S["d_rden_ready"], m + 1)
                    dve.wait_ge(S["d_z_free"], m + 1)
                    v.tensor_tensor(d_z.rearrange("p (h c) -> p h c", c=FO), acc[:, :, 0:FO],
                                    d_rden.unsqueeze(2).to_broadcast([P, HEADS, FO]), ALU.mult).then_inc(S["d_z_scaled"], 1)
                    dve.wait_ge(S["d_z_scaled"], m + 1)
                    v.tensor_tensor(d_z, d_z, x_all[:, bass.ds(m, 1), :].rearrange("p a f -> p (a f)"), ALU.add
                                    ).then_inc(S["d_z_ready"], 1)
                    dve.wait_ge(S["d_z_ready"], m + 1)


def kernel(x, adj, L0_gnn_weight, L0_gnn_att_src, L0_gnn_att_dst, L0_gnn_bias):
    import numpy as np
    import concourse.bacc as bacc
    from concourse.bass_utils import run_bass_kernel_spmd

    cols, n_const = const_layout(x.shape[0] // PACK)
    p = np.arange(P)
    consts = np.zeros((P, n_const), np.float32)
    eye = np.eye(P, dtype=np.float32)
    consts[:, slice(*cols["before"])] = p[:, None] < p[None, :]
    edges = np.tile(np.arange(EDGES, dtype=np.uint16), (P, 1))
    consts[:, slice(*cols["slot"])] = np.arange(SLOTS)
    consts[:, slice(*cols["edge_of"])] = np.arange(BLOCKS)[None, :] * P + p[:, None]
    consts[:, slice(*cols["pack"])] = (p[:, None] // PACK == np.arange(GPT)) * 2.0 ** (p[:, None] % PACK)
    masks = np.zeros((P, 2), np.uint32)
    masks[:, 0], masks[:, 1] = 0xFF800000, MANTISSA

    nc = bacc.Bacc("TRN2", target_bir_lowering=False, num_devices=1)
    host = {"x": x, "adj": adj, "weight": L0_gnn_weight, "att_src": L0_gnn_att_src, "att_dst": L0_gnn_att_dst,
            "bias": L0_gnn_bias, "eye": eye, "consts": consts, "edges": edges, "masks": masks}
    arrays, args = {}, []
    for name, a in host.items():
        a = np.ascontiguousarray(a)
        arrays[f"in_{name}"] = a
        args.append(nc.dram_tensor(f"in_{name}", a.shape, mybir.dt.from_np(a.dtype), kind="ExternalInput").ap())
    out = nc.dram_tensor("out", x.shape, mybir.dt.float32, kind="ExternalOutput").ap()
    gat_kernel(nc, *args, out)
    return run_bass_kernel_spmd(nc, [arrays], core_ids=[0]).results[0]["out"]
```

```python
from contextlib import ExitStack

import concourse.bass as bass
from concourse import mybir

F32 = mybir.dt.float32
BF16 = mybir.dt.bfloat16
U16 = mybir.dt.uint16
U32 = mybir.dt.uint32
I32 = mybir.dt.int32
ALU = mybir.AluOpType
ACT = mybir.ActivationFunctionType
AX_X = mybir.AxisListType.X

P = 128
HEADS = 4
EPS = 1e-5
SLOPE = 0.2

PACK = 16
GPT = P // PACK
TOP = 8
SLOTS = 2 * TOP
BITS = 3
BLOCKS = 6
EDGES = BLOCKS * P
PAIR = 2
LEAST = 2.0 ** -126
MOST = 3.4028234e38
BIAS_EXP = 127
MANTISSA = 23


class Steps:

    def __init__(self, sem, total, q, before=0):
        self.sem, self.base, self.n = sem, q * total + before, 0

    def mark(self, instruction):
        instruction.then_inc(self.sem, 1)
        self.n += 1
        return self.n

    def wait(self, engine, n=None):
        engine.wait_ge(self.sem, self.base + (self.n if n is None else n))


def const_layout(n_codes):
    widths = [("before", P), ("slot", SLOTS), ("edge_of", BLOCKS), ("pack", GPT)]
    at, cols = 0, {}
    for name, w in widths:
        cols[name] = (at, at + w)
        at += w
    return cols, at


def gat_kernel(nc, x, adj, weight, att_src, att_dst, bias, eye, consts, edges, masks, out, force_dense=False):
    N, F = x.shape
    T = N // P
    PAIRS = T // PAIR
    FO = F // HEADS
    ROW = HEADS + F
    VAL = F + HEADS
    EXT = ROW + HEADS
    CODES = N // PACK
    PG = 4
    GROUPS = T // PG
    RING = 8
    CHUNKS = RING // PAIR
    CT = T // CHUNKS
    HALVES = CHUNKS // PAIR
    NB = PAIR * BLOCKS
    C_OFF = SLOTS
    C_DST = C_OFF + 1
    C_HOT = C_DST + HEADS
    LW = C_HOT + P
    DC = 8
    DCHUNKS = T // DC
    IN_FLIGHT = 2
    X_PARTS = 4
    assert CODES == 512 and LW * 3 <= 512

    cols, n_const = const_layout(CODES)
    table = nc.dram_tensor("node_table", (N, ROW), F32, kind="Internal").ap()

    with ExitStack() as ctx:
        def sb(name, shape, dt=F32):
            return ctx.enter_context(nc.sbuf_tensor(name, shape, dt))

        def psum(name, shape, dt=F32):
            return ctx.enter_context(nc.psum_tensor(name, shape, dt))

        def sem(name):
            return ctx.enter_context(nc.semaphore(name))

        ring = sb("ring", [P, RING, CT, PAIR * P])
        x_all = sb("x_all", [P, T, F])
        const_sb = sb("const_sb", [P, n_const])
        edge_no_sb = sb("edge_no_sb", [P, EDGES], U16)
        edge_no = edge_no_sb[:, :]
        mask_sb = sb("mask_sb", [P, 2], U32)
        pack_w = sb("pack_w", [P, GPT], BF16)
        att_col = sb("att_col", [P, 2])
        alpha_dst = sb("alpha_dst", [P, T, HEADS])
        codes_left = sb("codes_left", [P, PAIR, CODES])
        top_code = sb("top_code", [P, PAIR, SLOTS])
        top_at = sb("top_at", [P, PAIR, SLOTS], U32)
        src_base = sb("src_base", [P, PAIR, SLOTS])
        bit = sb("bit", [P, BITS, PAIR, SLOTS])
        rest = sb("rest", [P, BITS, PAIR, SLOTS])
        bit_at = sb("bit_at", [P, BITS, PAIR, SLOTS], U32)
        cand_raw = sb("cand_raw", [P, BITS, PAIR, SLOTS])
        cand = sb("cand", [P, PAIR, BITS, SLOTS])
        cand_left = bit_at[:, :, :, :].rearrange("p k b s -> p (k b s)").bitcast(F32).rearrange(
            "p (b k s) -> p b k s", b=PAIR, k=BITS)
        is_src = sb("is_src", [P, PAIR, SLOTS])
        degree = sb("degree", [P, PAIR])
        lists = sb("lists", [P, 2, PAIR, LW])
        edge_end = sb("edge_end", [P, PAIR])
        over_slots = sb("over_slots", [P, PAIR])
        over_lists = sb("over_lists", [P, PAIR])
        least_degree = sb("least_degree", [P, PAIR])
        over_bits = sb("over_bits", [P, PAIR, SLOTS])
        over_edges = sb("over_edges", [P, PAIR])
        of_target = sb("of_target", [P, PAIR, EDGES])
        edge_rows = sb("edge_rows", [P, 2, NB, LW])
        place = sb("place", [P, NB])
        place_hot = sb("place_hot", [P, NB, SLOTS])
        src_next = sb("src_next", [P, NB])
        no_edge = sb("no_edge", [P, NB])
        most_tau = sb("most_tau", [P, 2, NB])
        src_idx = sb("src_idx", [P, 2, NB], U32)
        gathered = sb("gathered", [P, 2, NB, ROW + HEADS])
        logit = sb("logit", [P, NB, HEADS])
        tau = sb("tau", [P, NB, HEADS])
        rden = sb("rden", [P, PAIR, HEADS])
        z_out = sb("z_out", [P, PAIR, F])
        z_last = codes_left[:, 0, 0:PAIR * F].rearrange("p (b f) -> p b f", f=F)
        over = sb("over", [P, 5])
        over_any = sb("over_any", [P, 1])
        flag = sb("flag", [P, 1], I32)

        stats = edge_rows[:, 0, 0:3, :].rearrange("p a b -> p (a b)")[:, 0:T * 6].rearrange("p (t s) -> p t s", s=6)
        mean, mean_gap, rstd, var_eps, rstd_sq = (edge_rows[:, 0, 3 + k, 0:T] for k in range(5))
        x_norm = of_target[:, :, 0:PG * P].rearrange("p u (a f) -> p u a f", f=F)
        spare = edge_rows[:, 1].rearrange("p a b -> p (a b)")
        h_T = spare[:, 0:2 * PG * P].rearrange("p (u n) -> p u n", u=2)
        w_sb = spare[:, 1024:1024 + F]
        w_ext = spare[:, 1152:1152 + EXT]
        att_block = spare[:, 1288:1288 + 2 * HEADS]
        bias_sb = spare[:, 1296:1296 + F]
        ident = lists[:, 0, 0, C_HOT:LW]
        ones = of_target[:, 0, 0:P]
        gathered_all = gathered[:, :, :, :].rearrange("p u n c -> p (u n) c")
        table_rows = [gathered_all[:, w * PG:(w + 1) * PG, 0:ROW] for w in range(2 * NB // PG)]
        table_rows += [ap[:, 0:PG * ROW].rearrange("p (a c) -> p a c", c=ROW) for ap in
                       (codes_left[:, :, :].rearrange("p b c -> p (b c)"),
                        edge_rows[:, 0, 8:NB, :].rearrange("p n c -> p (n c)"))]
        ROW_BUFFERS = len(table_rows)
        CODES_ROWS, EDGES_ROWS = ROW_BUFFERS - 2, ROW_BUFFERS - 1

        ring_flat = ring[:, :, :, :].rearrange("p a b c -> p (a b c)")
        at = [0]

        def carve(*shape):
            n = 1
            for s in shape:
                n *= s
            ap = ring_flat[:, at[0]:at[0] + n]
            at[0] += n
            names = "abcd"[:len(shape)]
            if len(shape) == 1:
                return ap
            return ap.rearrange(f"p ({' '.join(names)}) -> p {' '.join(names)}", **dict(zip(names, shape)))

        d_adj = carve(2, DC, P)
        d_src = carve(2, DC, ROW)
        d_diag = carve(HEADS, P)
        d_dst = carve(HEADS, P)
        d_tau = carve(DC, HEADS, P)
        d_tau_flat = d_tau.rearrange("p a b c -> p (a b c)")
        d_acc = carve(VAL)
        d_rden = carve(HEADS)
        d_z = carve(F)

        ps_codes = psum("ps_codes", [P, 2, PAIR, CODES])
        ps_edge = psum("ps_edge", [P, 2, 512])
        ps_sum = psum("ps_sum", [P, 512])
        ps_misc = psum("ps_misc", [P, 512])

        def edge_view(ap):
            return ap[:, :, 0:3 * LW].rearrange("p k (b c) -> p k b c", c=LW)

        names = (
            "waits_held weights_in consts_in pack_ready "
            "att_zeroed att_ready projection_ready projection_kept moments_ready root_ready root_done rstd_ready "
            "normed turned relued projected rows_kept halves_kept rows_free biased "
            "codes_free decode degree_ready offset_done lists_done first_found of_target_ready edges_spread edges_kept "
            "place_steps idx_ready gathered0 gathered1 gathered_last logit_added logit_ready tau_ready tau_masked weighted "
            "summed rden_ready z_scaled z_ready z_stored "
            "over_zeroed over_ready ones_ready over_summed flag_ready "
            "d_adj0 d_adj1 d_src0 d_src1 d_diag_ready d_dst_done d_dst_kept d_logit d_exp d_tau_ready d_product d_added "
            "d_rden_ready d_z_scaled d_z_ready d_z_stored d_z_free").split()
        S = {n: sem(n) for n in names}
        ring_in = [sem(f"ring_in{k}") for k in range(RING)]
        ring_used = [sem(f"ring_used{k}") for k in range(RING)]
        rows_in = [sem(f"rows_in{w}") for w in range(ROW_BUFFERS)]
        x_in = [sem(f"x_in{k}") for k in range(X_PARTS)]
        LAST_GATHERED = ["gathered1", "gathered_last"]
        N_WEIGHT_DMAS = 4
        N_CONST_DMAS = 7

        block = ctx.enter_context(nc.Block())
        before = const_sb[:, cols["before"][0]:cols["before"][1]]
        slot_no = const_sb[:, cols["slot"][0]:cols["slot"][1]]
        edge_of = const_sb[:, cols["edge_of"][0]:cols["edge_of"][1]]
        pack_f = const_sb[:, cols["pack"][0]:cols["pack"][1]]

        def keep_half(copy, g, w, k):
            got = ps_edge[:, k, 0:2 * EXT].rearrange("p (a c) -> p a c", c=EXT)
            rows = table_rows[w][:, 2 * k:2 * k + 2, :]
            copy(rows, got[:, :, 0:ROW])
            at_tile = g * PG + 2 * k
            dst = alpha_dst[:, at_tile:at_tile + 2, :] if isinstance(g, int) else alpha_dst[:, bass.ds(at_tile, 2), :]
            return copy(dst, got[:, :, ROW:EXT])

        def lagged(i, u, lag):
            n = u - lag
            return i + n // 2, n % 2

        def tile_blocks(part):
            return slice(0, NB) if part is None else slice(part * BLOCKS, (part + 1) * BLOCKS)

        def tiles_of(part):
            return slice(0, PAIR) if part is None else slice(part, part + 1)

        def sums_of(part):
            if part is None:
                return ps_sum[:, 0:PAIR * VAL]
            return ps_edge[:, part, 0:VAL]

        def tile_chunk(k):
            return ring[:, k].rearrange("p t m -> p (t m)").rearrange("p (t m) -> p t m", m=P)

        def waited(engine):
            engine.sem_inc(S["waits_held"], 1)

        def slots(engine, slot, first, last, even_from, even_to):
            for s in range(first, even_from):
                slot(s // 2, s % 2, s)
            with engine.Fori(even_from // 2, even_to // 2) as i:
                for u in range(2):
                    slot(i, u, None)
            for s in range(even_to, last):
                slot(s // 2, s % 2, s)

        @block.sync
        def _(sp):
            sp.dma_start(lists[:, 0, 0, C_HOT:LW], eye).then_inc(S["weights_in"], 16)
            sp.dma_start(w_sb, weight).then_inc(S["weights_in"], 16)
            sp.dma_start(att_col[:, 0:1], att_src.rearrange("a h f -> (h f) a")).then_inc(S["weights_in"], 16)
            sp.dma_start(att_col[:, 1:2], att_dst.rearrange("a h f -> (h f) a")).then_inc(S["weights_in"], 16)
            for k in range(X_PARTS):
                tiles = slice(k * T // X_PARTS, (k + 1) * T // X_PARTS)
                sp.dma_start(x_all[:, tiles, :], x.rearrange("(t p) f -> p t f", p=P)[:, tiles, :]
                             ).then_inc(x_in[k], 16)
            sp.dma_start(const_sb[:, :], consts).then_inc(S["consts_in"], 16)
            sp.dma_start(edge_no, edges).then_inc(S["consts_in"], 16)
            sp.dma_start(mask_sb[:, :], masks).then_inc(S["consts_in"], 16)
            sp.dma_start(bias_sb, bias.rearrange("(a f) -> a f", a=1).to_broadcast([P, F])
                          ).then_inc(S["consts_in"], 16)
            for u in range(2):
                for b in range(PAIR):
                    if (u, b) != (0, 0):
                        sp.dma_start(lists[:, u, b, C_HOT:LW], eye).then_inc(S["consts_in"], 16)
            sp.sem_inc(S["edges_kept"], 1)
            sp.sem_inc(S["halves_kept"], 1)
            def load(i, k):
                u, c = k // CHUNKS, k % CHUNKS
                if k >= IN_FLIGHT:
                    sp.wait_ge(ring_in[k - IN_FLIGHT], i * 16 + 16)
                elif not isinstance(i, int):
                    sp.wait_ge(ring_in[k - IN_FLIGHT + RING], i * 16)
                at_target = (2 * i + u) * PAIR * P
                targets = slice(at_target, at_target + PAIR * P) if isinstance(i, int) else bass.ds(at_target, PAIR * P)
                sp.dma_start(ring[:, k], adj[c * CT * P:(c + 1) * CT * P, targets]
                             .rearrange("(t p) m -> p t m", p=P)).then_inc(ring_in[k], 16)

            for k in range(RING):
                load(0, k)
            with sp.Fori(1, PAIRS // 2 - 1) as i:
                for k in range(RING):
                    sp.wait_ge(ring_used[k], i)
                    waited(sp)
                    load(i, k)
            last_i = PAIRS // 2 - 1
            for k in range(CHUNKS):
                sp.wait_ge(ring_used[k], last_i)
                load(last_i, k)
            for b in range(PAIR):
                for c in range(HALVES):
                    k = CHUNKS + b * HALVES + c
                    sp.wait_ge(ring_used[k], last_i)
                    sp.wait_ge(ring_in[k - IN_FLIGHT], 16 * last_i + 16)
                    at_source, at_target = c * PAIR * CT * P, (T - PAIR + b) * P
                    sp.dma_start(tile_chunk(k), adj[at_source:at_source + PAIR * CT * P, at_target:at_target + P]
                                 .rearrange("(t p) m -> p t m", p=P)).then_inc(ring_in[k], 16)
            sp.wait_ge(S["z_stored"], 16 * (PAIRS + 1))
            sp.wait_ge(S["flag_ready"], 1)
            with sp.If(sp.value_load(flag[0:1, 0:1], min_val=0, max_val=P * 5) > 0):
                with sp.Fori(0, T) as m:
                    for c in range(DCHUNKS):
                        sp.wait_ge(S["d_product"], m * DCHUNKS + (c if c > 1 else 1))
                        sp.dma_start(d_adj[:, c % 2], adj[c * DC * P:(c + 1) * DC * P, bass.ds(m * P, P)]
                                     .rearrange("(t p) m -> p t m", p=P)).then_inc(S[f"d_adj{c % 2}"], 16)
                        sp.dma_start(d_src[:, c % 2], table[c * DC * P:(c + 1) * DC * P, :]
                                     .rearrange("(t p) c -> p t c", p=P)).then_inc(S[f"d_src{c % 2}"], 16)
                    sp.wait_ge(S["d_z_ready"], m + 1)
                    sp.dma_start(out[bass.ds(m * P, P), :], d_z).then_inc(S["d_z_stored"], 16)
                    sp.wait_ge(S["d_z_stored"], m * 16 + 16)
                    sp.sem_inc(S["d_z_free"], 1)

        @block.gpsimd
        def _(pool):
            pool.wait_ge(S["consts_in"], 16 * N_CONST_DMAS)
            with pool.Fori(0, GROUPS // ROW_BUFFERS) as i:
                for w in range(ROW_BUFFERS):
                    g = ROW_BUFFERS * i + w
                    pool.wait_ge(S["normed"], g + 1)
                    xs = x_all[:, bass.ds(g * PG, PG), :]
                    nc.gpsimd.tensor_tensor(xs, xs, bias_sb.unsqueeze(1).to_broadcast([P, PG, F]), ALU.add
                                            ).then_inc(S["biased"], 1)
                    pool.wait_ge(S["rows_kept"], g + 2)
                    pool.wait_ge(S["halves_kept"], g + 2)
                    pool.dma_start(table[bass.ds(g * PG * P, PG * P), :].rearrange("(a p) c -> p a c", p=P),
                                   table_rows[w]).then_inc(rows_in[w], 16)
            for w in range(ROW_BUFFERS):
                pool.wait_ge(rows_in[w], 16 * GROUPS // ROW_BUFFERS)
            def gather(i, u, part=None):
                q, n, own = 2 * i + u, part or 0, tile_blocks(part)
                pool.wait_ge(S["idx_ready"], q + (1 + n))
                pool.wait_ge(S["summed"], q + 1)
                waited(pool)
                for b in range(own.start, own.stop):
                    pool.indirect_dma_start(gathered[:, u, b, 0:ROW], None, table[:, :],
                                            bass.IndirectOffsetOnAxis(src_idx[:, u, b:b + 1], 0),
                                            bounds_check=N - 1, oob_is_err=False
                                            ).then_inc(S[LAST_GATHERED[part] if part is not None else f"gathered{u}"], 16)

            with pool.Fori(0, PAIRS // 2 - 1) as i:
                for u in range(2):
                    gather(i, u)
            gather(PAIRS // 2 - 1, 0)
            for b in range(PAIR):
                gather(PAIRS // 2 - 1, 1, b)

        @block.tensor
        def _(pe):
            pe.sem_inc(S["summed"], 2)
            pe.sem_inc(S["d_product"], 1)
            pe.wait_ge(S["weights_in"], 16 * N_WEIGHT_DMAS)
            pe.wait_ge(S["att_ready"], 1)
            pe.transpose(ps_misc[:, HEADS:ROW], w_sb, ident)
            pe.matmul(ps_misc[:, 0:HEADS], w_sb, att_block[:, 0:HEADS], start=True, stop=True)
            pe.matmul(ps_misc[:, ROW:EXT], w_sb, att_block[:, HEADS:], start=True, stop=True
                      ).then_inc(S["projection_ready"], 1)

            turned_at = [ps_sum, ps_misc]

            def turn(g, u):
                pe.wait_ge(S["normed"], g + 1)
                pe.wait_ge(S["relued"], g + 1)
                for a in range(PG):
                    last = pe.transpose(turned_at[u][:, a * P:(a + 1) * P], x_norm[:, u, a, :], ident)
                last.then_inc(S["turned"], 1)

            def project(g, u):
                pe.wait_ge(S["relued"], g + 3)
                pe.wait_ge(S["rows_kept"], g + 1)
                pe.wait_ge(S["halves_kept"], g + 1)
                for a in range(PG):
                    last = pe.matmul(ps_edge[:, a // 2, (a % 2) * EXT:(a % 2 + 1) * EXT], h_T[:, u, a * P:(a + 1) * P],
                                     w_ext, start=True, stop=True)
                last.then_inc(S["projected"], 1)

            def pack(i, u, c):
                q = 2 * i + u
                if c == 0:
                    pe.wait_ge(S["codes_free"], q + 1)
                k = u * CHUNKS + c
                pe.wait_ge(ring_in[k], 16 * i + 16)
                halves = ring[:, k].rearrange("p t m -> p (t m)").bitcast(BF16).rearrange(
                    "p (t b m e) -> p t b m e", b=PAIR, m=P, e=2)
                for b in range(PAIR):
                    for t in range(CT):
                        at_code = (c * CT + t) * GPT
                        last = pe.matmul(ps_codes[:, u, b, at_code:at_code + GPT], halves[:, t, b, :, 1],
                                         pack_w[:, :], start=True, stop=True)
                last.then_inc(ring_used[k], 1)

            def pack_tile(b, c):
                pe.wait_ge(S["codes_free"], PAIRS)
                k = CHUNKS + b * HALVES + c
                pe.wait_ge(ring_in[k], 16 * (PAIRS // 2))
                halves = ring[:, k].rearrange("p t m -> p (t m)").bitcast(BF16).rearrange(
                    "p (t m e) -> p t m e", m=P, e=2)
                for t in range(PAIR * CT):
                    at_code = (c * PAIR * CT + t) * GPT
                    last = pe.matmul(ps_codes[:, 1, b, at_code:at_code + GPT], halves[:, t, :, 1],
                                     pack_w[:, :], start=True, stop=True)
                last.then_inc(ring_used[k], 1)

            def offsets(i, u, part=None):
                q, n, tiles = 2 * i + u, part or 0, tiles_of(part)
                pe.wait_ge(S["degree_ready"], q + (1 + n))
                pe.wait_ge(S["lists_done"], q + (1 + n))
                pe.matmul(ps_misc[:, tiles], before, degree[:, tiles], start=True, stop=True
                          ).then_inc(S["offset_done"], 1)

            def spread(i, u, b):
                q = 2 * i + u
                pe.wait_ge(S["of_target_ready"], 2 * q + (b + 1))
                pe.wait_ge(S["edges_kept"], 2 * q + (b + 1))
                for e in range(BLOCKS):
                    last = pe.matmul(ps_edge[:, e // 3, (e % 3) * LW:(e % 3 + 1) * LW],
                                     of_target[:, b, e * P:(e + 1) * P], lists[:, u, b, :], start=True, stop=True)
                last.then_inc(S["edges_spread"], 1)

            def sum_edges(i, u, part=None):
                q, n, own = 2 * i + u, part or 0, tile_blocks(part)
                pe.wait_ge(S["weighted"], q + (1 + n))
                if part is None:
                    pe.wait_ge(S["z_scaled"], q + 1)
                else:
                    pe.wait_ge(S["edges_kept"], 2 * PAIRS + 1)
                sums = sums_of(part)
                for k, block in enumerate(range(own.start, own.stop)):
                    b, e = k // BLOCKS, k % BLOCKS
                    last = pe.matmul(sums[:, b * VAL:(b + 1) * VAL], edge_rows[:, u, block, C_HOT:LW],
                                     gathered[:, u, block, HEADS:], start=(e == 0), stop=(e == BLOCKS - 1))
                last.then_inc(S["summed"], 1)

            pe.wait_ge(S["projection_kept"], 1)
            turn(0, 0)
            for g in range(GROUPS):
                if g + 1 < GROUPS:
                    turn(g + 1, (g + 1) % 2)
                if g >= 1:
                    project(g - 1, (g - 1) % 2)
                if g == 2:
                    pe.wait_ge(S["pack_ready"], 1)
                if g >= 2 and g % 2 == 1:
                    at = (g - 3) // 2
                    pack(0, at // CHUNKS, at % CHUNKS)
            project(GROUPS - 1, 1)
            for at in range((GROUPS - 2) // 2, 2 * CHUNKS):
                pack(0, at // CHUNKS, at % CHUNKS)
            pe.wait_ge(S["rows_kept"], GROUPS + 1)
            pe.wait_ge(S["halves_kept"], GROUPS + 1)

            def sum_flags():
                pe.wait_ge(S["over_ready"], 1)
                pe.wait_ge(S["ones_ready"], 1)
                pe.matmul(ps_misc[:, 0:5], ones, over[:, :], start=True, stop=True).then_inc(S["over_summed"], 1)

            def slot(i, u, s):
                following, before_last = lagged(i, u, -1), lagged(i, u, 2)
                more, back = (s is None or s >= 1), (s is None or s >= 2)
                for c in range(CHUNKS):
                    if more:
                        pack(*following, c)
                    if c == 0:
                        offsets(i, u)
                    if c == 1 and back:
                        sum_edges(*before_last)
                for b in range(PAIR):
                    spread(i, u, b)

            slots(pe, slot, 0, PAIRS - 2, 2, PAIRS - 2)
            last_i = PAIRS // 2 - 1
            pack_tile(0, 0)
            offsets(last_i, 0)
            pack_tile(0, 1)
            sum_edges(last_i - 1, 0)
            pack_tile(1, 0)
            for b in range(PAIR):
                spread(last_i, 0, b)
            pack_tile(1, 1)
            offsets(last_i, 1, 0)
            sum_edges(last_i - 1, 1)
            spread(last_i, 1, 0)
            offsets(last_i, 1, 1)
            spread(last_i, 1, 1)
            sum_edges(last_i, 0)
            sum_edges(last_i, 1, 0)
            sum_flags()
            sum_edges(last_i, 1, 1)

            pe.wait_ge(S["flag_ready"], 1)
            with pe.If(pe.value_load(flag[0:1, 0:1], min_val=0, max_val=P * 5) > 0):
                with pe.Fori(0, T) as m:
                    pe.wait_ge(S["d_diag_ready"], m + 1)
                    pe.matmul(ps_misc[:, :], ones, d_diag.rearrange("p h m -> p (h m)"), start=True, stop=True
                              ).then_inc(S["d_dst_done"], 1)
                    for c in range(DCHUNKS):
                        k = m * DCHUNKS + c
                        pe.wait_ge(S["d_tau_ready"], k + 1)
                        pe.wait_ge(S["d_added"], k + 1)
                        for h in range(HEADS):
                            for t in range(DC):
                                last = pe.matmul(ps_sum[:, h * FO:(h + 1) * FO], d_tau[:, t, h, :],
                                                 d_src[:, c % 2, t, HEADS + h * FO:HEADS + (h + 1) * FO],
                                                 start=(t == 0), stop=(t == DC - 1))
                        for h in range(HEADS):
                            for t in range(DC):
                                last = pe.matmul(ps_sum[:, F + h:F + h + 1], d_tau[:, t, h, :], ones[:, 0:1],
                                                 start=(t == 0), stop=(t == DC - 1))
                        last.then_inc(S["d_product"], 1)

        @block.scalar
        def _(act):
            act.sem_inc(S["relued"], 2)
            act.wait_ge(S["projection_ready"], 1)
            nc.scalar.copy(w_ext, ps_misc[:, 0:EXT]).then_inc(S["projection_kept"], 1)
            act.wait_ge(S["root_ready"], 1)
            nc.scalar.activation(rstd, rstd, ACT.Sqrt).then_inc(S["root_done"], 1)
            turned_at = [ps_sum, ps_misc]
            with act.Fori(0, GROUPS // ROW_BUFFERS) as i:
                for w in range(ROW_BUFFERS):
                    g, u = ROW_BUFFERS * i + w, w % 2
                    act.wait_ge(S["turned"], g + 1)
                    act.wait_ge(S["projected"], g + 1)
                    nc.scalar.activation(h_T[:, u, :], turned_at[u][:, :], ACT.Relu).then_inc(S["relued"], 1)
                    act.wait_ge(S["projected"], g + 3)
                    act.wait_ge(S["rows_free"], g + 1)
                    keep_half(nc.scalar.copy, g, w, 0).then_inc(S["halves_kept"], 1)
            act.wait_ge(S["biased"], GROUPS)
            act.wait_ge(rows_in[EDGES_ROWS], 16 * GROUPS // ROW_BUFFERS)

            def keep_edges(i, u):
                q = 2 * i + u
                act.wait_ge(S["summed"], q + 1)
                for b in range(PAIR):
                    act.wait_ge(S["edges_spread"], 2 * q + (b + 1))
                    nc.scalar.copy(edge_rows[:, u, b * BLOCKS:(b + 1) * BLOCKS, :].rearrange("p (k b) c -> p k b c", k=2),
                                   edge_view(ps_edge)).then_inc(S["edges_kept"], 1)

            def exponentials(i, u, part=None):
                q, n, own = 2 * i + u, part or 0, tile_blocks(part)
                act.wait_ge(S["logit_ready"], q + (1 + n))
                nc.scalar.activation(tau[:, own, :], logit[:, own, :], ACT.Exp).then_inc(S["tau_ready"], 1)

            def store(i, u, part=None):
                q, n = 2 * i + u, part or 0
                act.wait_ge(S["z_ready"], q + (1 + n))
                tiles = tiles_of(part)
                first, count = (q * PAIR + n) * P, (tiles.stop - tiles.start) * P
                z = z_out if part is None else z_last
                rows = out[first:first + count, :] if isinstance(q, int) else out[bass.ds(first, count), :]
                act.dma_start(rows.rearrange("(b p) f -> p b f", p=P), z[:, tiles, :]).then_inc(S["z_stored"], 16)

            def slot(i, u, s):
                if s is None or s >= 3:
                    store(*lagged(i, u, 3))
                if s is None or s >= 2:
                    exponentials(*lagged(i, u, 2))
                keep_edges(i, u)

            slots(act, slot, 0, PAIRS, 4, PAIRS)
            last_i = PAIRS // 2 - 1
            store(last_i - 1, 1)
            exponentials(last_i, 0)
            exponentials(last_i, 1, 0)
            store(last_i, 0)
            exponentials(last_i, 1, 1)
            for b in range(PAIR):
                store(last_i, 1, b)

            act.wait_ge(S["flag_ready"], 1)
            with act.If(act.value_load(flag[0:1, 0:1], min_val=0, max_val=P * 5) > 0):
                with act.Fori(0, T) as m:
                    for c in range(DCHUNKS):
                        act.wait_ge(S["d_logit"], 2 * (m * DCHUNKS + c) + 2)
                        nc.scalar.activation(d_tau_flat, d_tau_flat, ACT.Exp).then_inc(S["d_exp"], 1)

        @block.vector
        def _(dve):
            dve.sem_inc(S["rows_kept"], 1)
            dve.sem_inc(S["projected"], 2)
            dve.sem_inc(S["codes_free"], 2)
            dve.sem_inc(S["lists_done"], 1)
            dve.sem_inc(S["z_scaled"], 1)
            dve.sem_inc(S["d_added"], 1)
            dve.sem_inc(S["d_z_free"], 1)
            v = nc.vector
            v.memset(att_block, 0.0).then_inc(S["att_zeroed"], 1)
            dve.wait_ge(S["att_zeroed"], 1)
            dve.wait_ge(S["weights_in"], 16 * N_WEIGHT_DMAS)
            for h in range(HEADS):
                for k in range(2):
                    last = v.tensor_copy(att_block[FO * h:FO * (h + 1), k * HEADS + h:k * HEADS + h + 1],
                                         att_col[FO * h:FO * (h + 1), k:k + 1])
            last.then_inc(S["att_ready"], 1)
            v.memset(over[:, :], 0.0)
            v.memset(over_slots[:, :], 0.0)
            v.memset(over_lists[:, :], 0.0)
            v.memset(least_degree[:, :], 1.0)
            v.memset(over_bits[:, :, :], 0.0)
            v.memset(over_edges[:, :], 0.0).then_inc(S["over_zeroed"], 1)
            for k in range(X_PARTS):
                dve.wait_ge(x_in[k], 16)
                for t in range(k * T // X_PARTS, (k + 1) * T // X_PARTS):
                    last = v.bn_stats(stats[:, t, :], x_all[:, t, :])
            m = Steps(S["moments_ready"], 6, 0)
            m.mark(last)
            m.wait(dve)
            mean_even, mean_odd, dev_even, dev_odd = (stats[:, :, k] for k in (1, 4, 2, 5))
            m.mark(v.tensor_tensor(mean_gap, mean_even, mean_odd, ALU.subtract))
            v.tensor_tensor(mean, mean_even, mean_odd, ALU.add)
            m.mark(v.tensor_tensor(var_eps, dev_even, dev_odd, ALU.add))
            m.wait(dve)
            m.mark(v.tensor_tensor(mean_gap, mean_gap, mean_gap, ALU.mult))
            v.tensor_scalar(mean, mean, 0.5, None, ALU.mult)
            m.mark(v.tensor_scalar(var_eps, var_eps, 1.0 / F, EPS, ALU.mult, ALU.add))
            m.wait(dve)
            m.mark(v.scalar_tensor_tensor(var_eps, mean_gap, 0.25, var_eps, ALU.mult, ALU.add))
            m.wait(dve)
            v.tensor_copy(rstd, var_eps).then_inc(S["root_ready"], 1)
            dve.wait_ge(S["consts_in"], 16 * N_CONST_DMAS)
            v.tensor_copy(pack_w[:, :], pack_f).then_inc(S["pack_ready"], 1)
            dve.wait_ge(S["root_done"], 1)
            r = Steps(S["rstd_ready"], 5, 0)
            r.mark(v.reciprocal(rstd, rstd))
            r.wait(dve)
            r.mark(v.tensor_tensor(rstd_sq, rstd, rstd, ALU.mult))
            r.wait(dve)
            r.mark(v.tensor_tensor(rstd_sq, rstd_sq, var_eps, ALU.mult))
            r.wait(dve)
            r.mark(v.tensor_scalar(rstd_sq, rstd_sq, -0.5, 1.5, ALU.mult, ALU.add))
            r.wait(dve)
            r.mark(v.tensor_tensor(rstd, rstd, rstd_sq, ALU.mult))
            r.wait(dve)

            def normalise(g, u):
                for a in range(PG):
                    t = g * PG + a
                    one = (lambda ap: ap[:, bass.ds(t, 1)]) if not isinstance(t, int) else (lambda ap: ap[:, t:t + 1])
                    last = v.tensor_scalar(x_norm[:, u, a, :], one(x_all[:, :, :]).rearrange("p a f -> p (a f)"),
                                           one(mean), one(rstd), ALU.subtract, ALU.mult)
                last.then_inc(S["normed"], 1)

            def keep_rows(g, u):
                keep_half(v.tensor_copy, g, g % ROW_BUFFERS, 1).then_inc(S["rows_kept"], 1)

            for g in range(2):
                normalise(g, g)
            dve.sem_inc(S["rows_free"], ROW_BUFFERS)
            for g in range(GROUPS):
                u = g % 2
                if g + 2 < GROUPS:
                    dve.wait_ge(S["turned"], g + 1)
                    normalise(g + 2, u)
                dve.wait_ge(S["projected"], g + 3)
                if g >= ROW_BUFFERS:
                    dve.wait_ge(rows_in[g % ROW_BUFFERS], 16 * (g // ROW_BUFFERS))
                    dve.sem_inc(S["rows_free"], 1)
                keep_rows(g, u)
            dve.wait_ge(rows_in[CODES_ROWS], 16 * GROUPS // ROW_BUFFERS)
            dve.wait_ge(S["over_zeroed"], 1)

            E_STEPS, TILE_STEPS = 25, 17

            def find_codes(i, u, part=None):
                q, n = 2 * i + u, part or 0
                st = Steps(S["decode"], E_STEPS, q, n * TILE_STEPS)
                for k in range(CHUNKS) if part is None else range(part * HALVES, (part + 1) * HALVES):
                    dve.wait_ge(ring_used[u * CHUNKS + k], i + 1)
                both = range(PAIR) if part is None else [part]
                codes = {b: ps_codes[:, u, b, :] for b in both}
                first = {b: top_code[:, b, 0:TOP] for b in both}
                second = {b: top_code[:, b, TOP:SLOTS] for b in both}
                waited(dve)
                for b in both:
                    st.mark(v.max(first[b], codes[b]))
                st.wait(dve)
                waited(dve)
                for b in both:
                    st.mark(v.max_index(top_at[:, b, 0:TOP], first[b], codes[b]))
                for b in both:
                    last = v.match_replace(codes_left[:, b, :], first[b], codes[b], 0.0)
                last.then_inc(S["codes_free"], 1)
                dve.wait_ge(S["codes_free"], q + (3 + n))
                waited(dve)
                for b in both:
                    st.mark(v.max(second[b], codes_left[:, b, :]))
                st.wait(dve)
                waited(dve)
                for b in both:
                    st.mark(v.max_index(top_at[:, b, TOP:SLOTS], second[b], codes_left[:, b, :]))
                return st

            def decode(i, u, st, part=None):
                q, n, tiles = 2 * i + u, part or 0, tiles_of(part)
                both = range(tiles.start, tiles.stop)
                count = len(both)
                if not isinstance(q, int) or q >= 2:
                    dve.wait_ge(S["edges_spread"], 2 * q - 2)

                def levels(ap):
                    return ap[:, :, tiles, :].rearrange("p k b s -> p k (b s)")

                mask = mask_sb[:, 0:1].unsqueeze(2).to_broadcast([P, count, SLOTS])
                left = top_code[:, tiles, :]
                for k in range(BITS):
                    st.mark(v.tensor_tensor(bit[:, k, tiles].bitcast(U32), left.bitcast(U32), mask, ALU.bitwise_and))
                    if k == 1:
                        st.mark(v.tensor_scalar(src_base[:, tiles, :], top_at[:, tiles, :], float(PACK),
                                                float(1 - BIAS_EXP), ALU.mult, ALU.add))
                        st.wait(dve, st.n - 1)
                    else:
                        st.wait(dve)
                    st.mark(v.tensor_tensor(rest[:, k, tiles], left, bit[:, k, tiles], ALU.subtract))
                    if k < BITS - 1:
                        st.wait(dve)
                    left = rest[:, k, tiles]
                st.mark(v.tensor_tensor(levels(bit_at), levels(bit).bitcast(U32),
                                        mask_sb[:, 1:2].unsqueeze(2).to_broadcast([P, BITS, count * SLOTS]),
                                        ALU.logical_shift_right))
                st.wait(dve)
                st.mark(v.tensor_tensor(levels(cand_raw), levels(bit_at),
                                        src_base[:, tiles, :].rearrange("p b s -> p (b s)").unsqueeze(1)
                                        .to_broadcast([P, BITS, count * SLOTS]), ALU.add))
                st.wait(dve)
                for b in both:
                    st.mark(v.scalar_tensor_tensor(cand[:, b], bit[:, :, b, :], 0.0, cand_raw[:, :, b, :],
                                                   ALU.is_gt, ALU.mult))
                st.wait(dve)
                waited(dve)
                flat = {b: cand[:, b].rearrange("p k s -> p (k s)") for b in both}
                flat_left = {b: cand_left[:, b].rearrange("p k s -> p (k s)") for b in both}
                for b in both:
                    st.mark(v.max(lists[:, u, b, 0:TOP], flat[b]))
                st.wait(dve)
                waited(dve)
                for b in both:
                    st.mark(v.match_replace(flat_left[b], lists[:, u, b, 0:TOP], flat[b], 0.0))
                st.wait(dve)
                waited(dve)
                for b in both:
                    st.mark(v.max(lists[:, u, b, TOP:SLOTS], flat_left[b]))
                st.wait(dve)
                assert st.n == (E_STEPS if part is None else TILE_STEPS)
                v.tensor_scalar(is_src[:, tiles, :], lists[:, u, tiles, 0:SLOTS], 0.0, None, ALU.is_gt
                                ).then_inc(S["first_found"], 1)
                dve.wait_ge(S["first_found"], 3 * q + (1 + 2 * n))
                v.tensor_reduce(degree[:, tiles], is_src[:, tiles, :], AX_X, ALU.add).then_inc(S["degree_ready"], 1)
                dve.wait_ge(S["degree_ready"], q + (1 + n))
                v.tensor_tensor(over_slots[:, tiles], over_slots[:, tiles], top_code[:, tiles, SLOTS - 1], ALU.max)
                v.tensor_tensor(least_degree[:, tiles], least_degree[:, tiles], degree[:, tiles], ALU.min)
                v.tensor_tensor(over_bits[:, tiles, :], over_bits[:, tiles, :], rest[:, BITS - 1, tiles], ALU.max)

            def list_edges(i, u, part=None):
                q, n, tiles = 2 * i + u, part or 0, tiles_of(part)
                both = range(tiles.start, tiles.stop)
                dve.wait_ge(S["offset_done"], q + (1 + n))
                v.tensor_copy(lists[:, u, tiles, C_OFF], ps_misc[:, tiles])
                v.tensor_tensor(edge_end[:, tiles], ps_misc[:, tiles], degree[:, tiles], ALU.add
                                ).then_inc(S["lists_done"], 1)
                at_tile = q * PAIR + n
                v.tensor_copy(lists[:, u, tiles, C_DST:C_DST + HEADS],
                              alpha_dst[:, at_tile:at_tile + len(both), :] if isinstance(q, int) else
                              alpha_dst[:, bass.ds(at_tile, len(both)), :])
                v.tensor_tensor(over_lists[:, tiles], over_lists[:, tiles], lists[:, u, tiles, SLOTS - 1], ALU.max)
                dve.wait_ge(S["lists_done"], q + (2 + n))
                if not isinstance(q, int) or q >= 1:
                    dve.wait_ge(S["edges_spread"], 2 * q)
                v.tensor_tensor(over_edges[:, tiles], over_edges[:, tiles], edge_end[:, tiles], ALU.max)
                for b in both:
                    v.tensor_scalar(of_target[:, b, :], edge_no, lists[:, u, b, C_OFF:C_OFF + 1], None, ALU.is_ge
                                    ).then_inc(S["first_found"], 1)
                    dve.wait_ge(S["first_found"], 3 * q + (2 + (b if part is None else 2 * b)))
                    v.scalar_tensor_tensor(of_target[:, b, :], edge_no, edge_end[:, b:b + 1], of_target[:, b, :],
                                           ALU.is_lt, ALU.mult).then_inc(S["of_target_ready"], 1)
                    dve.wait_ge(S["of_target_ready"], 2 * q + (b + 1))

            def pick_sources(i, u, part=None):
                q, n = 2 * i + u, part or 0
                own = tile_blocks(part)
                count = own.stop - own.start
                st = Steps(S["place_steps"], 5, q + n)
                dve.wait_ge(S["edges_kept"], 2 * q + (3 if part is None else 2 + part))
                if not isinstance(q, int) or q >= 2:
                    dve.wait_ge(S[f"gathered{u}"], i * (16 * NB))
                got = edge_rows[:, u, own]
                st.mark(v.tensor_tensor(place[:, own].rearrange("p (b e) -> p b e", e=BLOCKS),
                                        edge_of.unsqueeze(1).to_broadcast([P, count // BLOCKS, BLOCKS]),
                                        got[:, :, C_OFF].rearrange("p (b e) -> p b e", e=BLOCKS), ALU.subtract))
                st.wait(dve)
                hot = place_hot[:, own, :]
                st.mark(v.tensor_tensor(hot, slot_no.unsqueeze(1).to_broadcast([P, count, SLOTS]),
                                        place[:, own].unsqueeze(2).to_broadcast([P, count, SLOTS]), ALU.is_equal))
                st.wait(dve)
                st.mark(v.tensor_tensor(hot, hot, got[:, :, 0:SLOTS], ALU.mult))
                st.wait(dve)
                st.mark(v.tensor_reduce(src_next[:, own], hot, AX_X, ALU.add))
                st.wait(dve)
                st.mark(v.tensor_scalar(no_edge[:, own], src_next[:, own], 0.5, float(2 * N), ALU.is_lt, ALU.mult))
                v.tensor_scalar(most_tau[:, u, own], src_next[:, own], 0.5, MOST, ALU.is_gt, ALU.mult)
                st.wait(dve)
                v.scalar_tensor_tensor(src_idx[:, u, own], src_next[:, own], -1.0, no_edge[:, own], ALU.add, ALU.add
                                       ).then_inc(S["idx_ready"], 1)

            def logits(i, u, part=None):
                q, n, own = 2 * i + u, part or 0, tile_blocks(part)
                if part is None:
                    dve.wait_ge(S[f"gathered{u}"], i * (16 * NB) + 16 * NB)
                else:
                    dve.wait_ge(S[LAST_GATHERED[part]], i * (16 * NB) * (1 - part) + 16 * BLOCKS)
                v.tensor_tensor(logit[:, own, :], gathered[:, u, own, 0:HEADS], edge_rows[:, u, own, C_DST:C_DST + HEADS],
                                ALU.add).then_inc(S["logit_added"], 1)
                dve.wait_ge(S["logit_added"], q + (1 + n))
                v.scalar_tensor_tensor(logit[:, own, :], logit[:, own, :], SLOPE, logit[:, own, :], ALU.mult, ALU.max
                                       ).then_inc(S["logit_ready"], 1)

            def weigh(i, u, part=None):
                q, n, own = 2 * i + u, part or 0, tile_blocks(part)
                count = own.stop - own.start
                dve.wait_ge(S["tau_ready"], q + (1 + n))
                weight_of = gathered[:, u, own, ROW:]
                v.tensor_tensor(weight_of, tau[:, own, :], most_tau[:, u, own].unsqueeze(2).to_broadcast([P, count, HEADS]),
                                ALU.min).then_inc(S["tau_masked"], 1)
                dve.wait_ge(S["tau_masked"], q + (1 + n))
                rows = gathered[:, u, own, HEADS:ROW].rearrange("p e (h c) -> p e h c", c=FO)
                v.tensor_tensor(rows, rows, weight_of.unsqueeze(3).to_broadcast([P, count, HEADS, FO]), ALU.mult
                                ).then_inc(S["weighted"], 1)

            def finish(i, u, part=None):
                q, n = 2 * i + u, part or 0
                dve.wait_ge(S["summed"], q + (3 + n))
                tiles = tiles_of(part)
                count = tiles.stop - tiles.start
                z = z_out if part is None else z_last
                sums = sums_of(part).rearrange("p (b c) -> p b c", c=VAL)
                v.tensor_scalar(rden[:, tiles, :], sums[:, :, F:], LEAST, None, ALU.max).then_inc(S["rden_ready"], 1)
                dve.wait_ge(S["rden_ready"], 2 * q + (1 + 2 * n))
                v.reciprocal(rden[:, tiles, :], rden[:, tiles, :]).then_inc(S["rden_ready"], 1)
                if part is None and (not isinstance(q, int) or q >= 1):
                    dve.wait_ge(S["z_stored"], q * 16)
                dve.wait_ge(S["rden_ready"], 2 * q + (2 + 2 * n))
                v.tensor_tensor(z[:, tiles, :].rearrange("p b (h c) -> p b h c", c=FO),
                                sums[:, :, 0:F].rearrange("p b (h c) -> p b h c", c=FO),
                                rden[:, tiles, :].unsqueeze(3).to_broadcast([P, count, HEADS, FO]), ALU.mult
                                ).then_inc(S["z_scaled"], 1)
                dve.wait_ge(S["z_scaled"], q + (2 + n))
                at_tile = q * PAIR + n
                xs = x_all[:, bass.ds(at_tile, PAIR), :] if not isinstance(q, int) else x_all[:, at_tile:at_tile + count, :]
                v.tensor_tensor(z[:, tiles, :], z[:, tiles, :], xs, ALU.add).then_inc(S["z_ready"], 1)

            def sum_overs():
                v.tensor_reduce(over[:, 0:1], over_slots[:, :], AX_X, ALU.max)
                v.tensor_reduce(over[:, 1:2], over_bits[:, :, :].rearrange("p b s -> p (b s)"), AX_X, ALU.max)
                v.tensor_reduce(over[:, 2:3], over_lists[:, :], AX_X, ALU.max)
                v.tensor_reduce(over[:, 3:4], over_edges[:, :], AX_X, ALU.max)
                v.tensor_reduce(over[:, 4:5], least_degree[:, :], AX_X, ALU.min).then_inc(S["over_zeroed"], 1)
                dve.wait_ge(S["edges_spread"], 2 * PAIRS)
                v.memset(ones, 1.0).then_inc(S["ones_ready"], 1)
                dve.wait_ge(S["over_zeroed"], 2)
                v.tensor_scalar(over[:, 0:3], over[:, 0:3], 0.0, None, ALU.is_gt)
                v.tensor_scalar(over[:, 4:5], over[:, 4:5], 0.5, None, ALU.is_lt)
                v.tensor_scalar(over[:, 3:4], over[:, 3:4], float(EDGES if not force_dense else 0), None, ALU.is_gt
                                ).then_inc(S["over_ready"], 1)

            def raise_flag():
                dve.wait_ge(S["over_summed"], 1)
                v.tensor_reduce(over_any[:, :], ps_misc[:, 0:5], AX_X, ALU.add).then_inc(S["over_zeroed"], 1)
                dve.wait_ge(S["over_zeroed"], 3)
                v.tensor_copy(flag[:, :], over_any[:, :]).then_inc(S["flag_ready"], 1)

            def slot(i, u, s):
                decode(i, u, find_codes(i, u))
                if s is None or s >= 1:
                    pick_sources(*lagged(i, u, 1))
                if s is None or s >= 3:
                    finish(*lagged(i, u, 3))
                if s is None or s >= 2:
                    logits(*lagged(i, u, 2))
                    weigh(*lagged(i, u, 2))
                list_edges(i, u)

            dve.wait_ge(S["biased"], GROUPS)
            slots(dve, slot, 0, PAIRS - 2, 4, PAIRS - 2)
            slot(PAIRS // 2 - 1, 0, PAIRS - 2)
            i = PAIRS // 2 - 1
            steps = find_codes(i, 1, 0)
            finish(i - 1, 0)
            decode(i, 1, steps, 0)
            logits(i - 1, 1)
            pick_sources(i, 0)
            weigh(i - 1, 1)
            list_edges(i, 1, 0)
            steps = find_codes(i, 1, 1)
            decode(i, 1, steps, 1)
            pick_sources(i, 1, 0)
            list_edges(i, 1, 1)
            finish(i - 1, 1)
            logits(i, 0)
            pick_sources(i, 1, 1)
            weigh(i, 0)
            sum_overs()
            logits(i, 1, 0)
            weigh(i, 1, 0)
            finish(i, 0)
            raise_flag()
            logits(i, 1, 1)
            weigh(i, 1, 1)
            for b in range(PAIR):
                finish(i, 1, b)

            dve.wait_ge(S["flag_ready"], 1)
            with dve.If(dve.value_load(flag[0:1, 0:1], min_val=0, max_val=P * 5) > 0):
                with dve.Fori(0, T) as m:
                    v.tensor_tensor(d_diag, ident.unsqueeze(1).to_broadcast([P, HEADS, P]),
                                    alpha_dst[:, bass.ds(m, 1), :].rearrange("p a h -> p (a h)").unsqueeze(2)
                                    .to_broadcast([P, HEADS, P]), ALU.mult).then_inc(S["d_diag_ready"], 1)
                    v.memset(d_acc, 0.0)
                    dve.wait_ge(S["d_dst_done"], m + 1)
                    v.tensor_copy(d_dst.rearrange("p h m -> p (h m)"), ps_misc[:, :]).then_inc(S["d_dst_kept"], 1)
                    dve.wait_ge(S["d_dst_kept"], m + 1)
                    for c in range(DCHUNKS):
                        k = m * DCHUNKS + c
                        dve.wait_ge(S[f"d_adj{c % 2}"], m * (8 * DCHUNKS) + 16 * (c // 2 + 1))
                        dve.wait_ge(S[f"d_src{c % 2}"], m * (8 * DCHUNKS) + 16 * (c // 2 + 1))
                        v.tensor_tensor(d_tau, d_dst.unsqueeze(1).to_broadcast([P, DC, HEADS, P]),
                                        d_src[:, c % 2, :, 0:HEADS].unsqueeze(3).to_broadcast([P, DC, HEADS, P]), ALU.add
                                        ).then_inc(S["d_logit"], 1)
                        dve.wait_ge(S["d_logit"], 2 * k + 1)
                        v.scalar_tensor_tensor(d_tau_flat, d_tau_flat, SLOPE, d_tau_flat, ALU.mult, ALU.max
                                               ).then_inc(S["d_logit"], 1)
                        dve.wait_ge(S["d_exp"], k + 1)
                        v.tensor_tensor(d_tau, d_tau, d_adj[:, c % 2].unsqueeze(2).to_broadcast([P, DC, HEADS, P]), ALU.mult
                                        ).then_inc(S["d_tau_ready"], 1)
                        dve.wait_ge(S["d_product"], k + 2)
                        v.tensor_tensor(d_acc, d_acc, ps_sum[:, 0:VAL], ALU.add).then_inc(S["d_added"], 1)
                        dve.wait_ge(S["d_added"], k + 2)
                    v.reciprocal(d_rden, d_acc[:, F:]).then_inc(S["d_rden_ready"], 1)
                    dve.wait_ge(S["d_rden_ready"], m + 1)
                    dve.wait_ge(S["d_z_free"], m + 1)
                    v.tensor_tensor(d_z.rearrange("p (h c) -> p h c", c=FO), d_acc[:, 0:F].rearrange("p (h c) -> p h c", c=FO),
                                    d_rden.unsqueeze(2).to_broadcast([P, HEADS, FO]), ALU.mult).then_inc(S["d_z_scaled"], 1)
                    dve.wait_ge(S["d_z_scaled"], m + 1)
                    v.tensor_tensor(d_z, d_z, x_all[:, bass.ds(m, 1), :].rearrange("p a f -> p (a f)"), ALU.add
                                    ).then_inc(S["d_z_ready"], 1)
                    dve.wait_ge(S["d_z_ready"], m + 1)


def kernel(x, adj, L0_gnn_weight, L0_gnn_att_src, L0_gnn_att_dst, L0_gnn_bias):
    import numpy as np
    import concourse.bacc as bacc
    from concourse.bass_utils import run_bass_kernel_spmd

    cols, n_const = const_layout(x.shape[0] // PACK)
    p = np.arange(P)
    consts = np.zeros((P, n_const), np.float32)
    eye = np.eye(P, dtype=np.float32)
    consts[:, slice(*cols["before"])] = p[:, None] < p[None, :]
    edges = np.tile(np.arange(EDGES, dtype=np.uint16), (P, 1))
    consts[:, slice(*cols["slot"])] = np.arange(SLOTS)
    consts[:, slice(*cols["edge_of"])] = np.arange(BLOCKS)[None, :] * P + p[:, None]
    consts[:, slice(*cols["pack"])] = (p[:, None] // PACK == np.arange(GPT)) * 2.0 ** (p[:, None] % PACK)
    masks = np.zeros((P, 2), np.uint32)
    masks[:, 0], masks[:, 1] = 0xFF800000, MANTISSA

    nc = bacc.Bacc("TRN2", target_bir_lowering=False, num_devices=1)
    host = {"x": x, "adj": adj, "weight": L0_gnn_weight, "att_src": L0_gnn_att_src, "att_dst": L0_gnn_att_dst,
            "bias": L0_gnn_bias, "eye": eye, "consts": consts, "edges": edges, "masks": masks}
    arrays, args = {}, []
    for name, a in host.items():
        a = np.ascontiguousarray(a)
        arrays[f"in_{name}"] = a
        args.append(nc.dram_tensor(f"in_{name}", a.shape, mybir.dt.from_np(a.dtype), kind="ExternalInput").ap())
    out = nc.dram_tensor("out", x.shape, mybir.dt.float32, kind="ExternalOutput").ap()
    gat_kernel(nc, *args, out)
    return run_bass_kernel_spmd(nc, [arrays], core_ids=[0]).results[0]["out"]
```
